# Optimizing a Trainium2 kernel written in Bass

```python
import numpy as np
import jax
import jax.numpy as jnp

def _softmax(x, axis=-1):
    return jax.nn.softmax(x, axis=axis)

def _gelu(x):
    return jax.nn.gelu(x, approximate=True)

def _silu(x):
    return jax.nn.silu(x)

def _sigmoid(x):
    return jax.nn.sigmoid(x)

def _layernorm(x, axis=-1, eps=1e-05):
    m = jnp.mean(x, axis=axis, keepdims=True)
    v = jnp.var(x, axis=axis, keepdims=True)
    return (x - m) / jnp.sqrt(v + eps)

def _scatter_add(tgt, idx, src, axis=0):
    return tgt.at[idx].add(src)

def _segment_sum(src, seg, n):
    return jax.ops.segment_sum(src, seg, n)
kernel_name = 'mk_adj_ffn_d1_adj_r2_4e2648'

def setup_inputs(seed: int=0):
    np.random.seed(seed)
    _w = jnp.asarray

    def _rec_inputs():
        import jax
        import jax.numpy as jnp
        _gk = jax.random.key(seed)
        x = 7.22e-05 + 1 * jax.random.normal(jax.random.fold_in(_gk, 1), (32, 256, 128), jnp.float32)
        _a = jax.random.bernoulli(jax.random.fold_in(_gk, 2), 0.0625, (32, 256, 256))
        _a = jnp.logical_or(_a, jnp.swapaxes(_a, -1, -2))
        _a = jnp.logical_or(_a, jnp.eye(256, dtype=bool))
        _af = _a.astype(jnp.float32)
        adj = _af
        return (x, adj)
    x, adj = _rec_inputs()

    def _L0_gnn_setup():
        import jax, jax.numpy as jnp
        import numpy as np
        from jax import lax
        DIM = 128
        EPS = 1e-05

        def _bn(h, g, b, m, v):
            scale = g / jnp.sqrt(v + EPS)
            return h * scale[None, :, None] + (b - m * scale)[None, :, None]

        def _conv1d(h, w, pad):
            return lax.conv_general_dilated(h, w, window_strides=(1,), padding=[(pad, pad)], dimension_numbers=('NCH', 'OIH', 'NCH'))
        key = jax.random.key(seed)
        ks = jax.random.split(key, 16)
        bs, n, d = (16, 1024, DIM)
        s = 0.05
        return {'x': jax.random.normal(ks[0], (bs, n, d), jnp.float32), 'mask': jnp.ones((bs, n, n), jnp.float32), 'w_se': jax.random.normal(ks[1], (3, d), jnp.float32) * s, 'b_se': jnp.zeros((3,), jnp.float32), 'conv1_w': jax.random.normal(ks[2], (d, d, 1), jnp.float32) * s, 'bn1_g': jnp.ones((d,), jnp.float32), 'bn1_b': jnp.zeros((d,), jnp.float32), 'bn1_m': jnp.zeros((d,), jnp.float32), 'bn1_v': jnp.ones((d,), jnp.float32), 'conv2_w': jax.random.normal(ks[3], (d, d, 17), jnp.float32) * s, 'bn2_g': jnp.ones((d,), jnp.float32), 'bn2_b': jnp.zeros((d,), jnp.float32), 'bn2_m': jnp.zeros((d,), jnp.float32), 'bn2_v': jnp.ones((d,), jnp.float32), 'w_msg': jax.random.normal(ks[4], (d, d), jnp.float32) * s, 'b_msg': jnp.zeros((d,), jnp.float32), 'w_ih': jax.random.normal(ks[5], (3 * d, 2 * d), jnp.float32) * s, 'b_ih': jnp.zeros((3 * d,), jnp.float32), 'w_hh': jax.random.normal(ks[6], (3 * d, d), jnp.float32) * s, 'b_hh': jnp.zeros((3 * d,), jnp.float32)}
    _L0_gnn_all = _L0_gnn_setup()
    _L0_gnn_in = {k: v for k, v in _L0_gnn_all.items() if k in ('w_se', 'b_se', 'conv1_w', 'bn1_g', 'bn1_b', 'bn1_m', 'bn1_v', 'conv2_w', 'bn2_g', 'bn2_b', 'bn2_m', 'bn2_v', 'w_msg', 'b_msg', 'w_ih', 'b_ih', 'w_hh', 'b_hh')}
    del _L0_gnn_all

    def _L0_ffn_setup():
        import jax, jax.numpy as jnp
        import numpy as np
        B, S, D, E, H, K = (4, 2048, 128, 8, 256, 2)
        key = jax.random.key(seed)
        ks = jax.random.split(key, 6)
        x = jax.random.normal(ks[0], (B, S, D), jnp.float32)
        Wg = jax.random.normal(ks[1], (D, E), jnp.float32) * 0.02
        bg = jnp.zeros((E,), jnp.float32)
        W1 = jax.random.normal(ks[2], (E, D, H), jnp.float32) * 0.02
        b1 = jnp.zeros((E, H), jnp.float32)
        W2 = jax.random.normal(ks[3], (E, H, D), jnp.float32) * 0.02
        b2 = jnp.zeros((E, D), jnp.float32)
        return {'x': x, 'Wg': Wg, 'bg': bg, 'W1': W1, 'b1': b1, 'W2': W2, 'b2': b2}
    _L0_ffn_all = _L0_ffn_setup()
    _L0_ffn_in = {k: v for k, v in _L0_ffn_all.items() if k in ('Wg', 'bg', 'W1', 'b1', 'W2', 'b2')}
    del _L0_ffn_all
    return {'x': x, 'adj': adj, 'L0_gnn_w_se': _L0_gnn_in['w_se'], 'L0_gnn_b_se': _L0_gnn_in['b_se'], 'L0_gnn_conv1_w': _L0_gnn_in['conv1_w'], 'L0_gnn_bn1_g': _L0_gnn_in['bn1_g'], 'L0_gnn_bn1_b': _L0_gnn_in['bn1_b'], 'L0_gnn_bn1_m': _L0_gnn_in['bn1_m'], 'L0_gnn_bn1_v': _L0_gnn_in['bn1_v'], 'L0_gnn_conv2_w': _L0_gnn_in['conv2_w'], 'L0_gnn_bn2_g': _L0_gnn_in['bn2_g'], 'L0_gnn_bn2_b': _L0_gnn_in['bn2_b'], 'L0_gnn_bn2_m': _L0_gnn_in['bn2_m'], 'L0_gnn_bn2_v': _L0_gnn_in['bn2_v'], 'L0_gnn_w_msg': _L0_gnn_in['w_msg'], 'L0_gnn_b_msg': _L0_gnn_in['b_msg'], 'L0_gnn_w_ih': _L0_gnn_in['w_ih'], 'L0_gnn_b_ih': _L0_gnn_in['b_ih'], 'L0_gnn_w_hh': _L0_gnn_in['w_hh'], 'L0_gnn_b_hh': _L0_gnn_in['b_hh'], 'L0_ffn_Wg': _L0_ffn_in['Wg'], 'L0_ffn_bg': _L0_ffn_in['bg'], 'L0_ffn_W1': _L0_ffn_in['W1'], 'L0_ffn_b1': _L0_ffn_in['b1'], 'L0_ffn_W2': _L0_ffn_in['W2'], 'L0_ffn_b2': _L0_ffn_in['b2']}

def reference(x, adj, L0_gnn_w_se, L0_gnn_b_se, L0_gnn_conv1_w, L0_gnn_bn1_g, L0_gnn_bn1_b, L0_gnn_bn1_m, L0_gnn_bn1_v, L0_gnn_conv2_w, L0_gnn_bn2_g, L0_gnn_bn2_b, L0_gnn_bn2_m, L0_gnn_bn2_v, L0_gnn_w_msg, L0_gnn_b_msg, L0_gnn_w_ih, L0_gnn_b_ih, L0_gnn_w_hh, L0_gnn_b_hh, L0_ffn_Wg, L0_ffn_bg, L0_ffn_W1, L0_ffn_b1, L0_ffn_W2, L0_ffn_b2):
    import jax
    import jax.numpy as jnp

    def _L0_gnn_ref(x, mask, w_se, b_se, conv1_w, bn1_g, bn1_b, bn1_m, bn1_v, conv2_w, bn2_g, bn2_b, bn2_m, bn2_v, w_msg, b_msg, w_ih, b_ih, w_hh, b_hh):
        import jax, jax.numpy as jnp
        import numpy as np
        from jax import lax
        DIM = 128
        EPS = 1e-05

        def _bn(h, g, b, m, v):
            scale = g / jnp.sqrt(v + EPS)
            return h * scale[None, :, None] + (b - m * scale)[None, :, None]

        def _conv1d(h, w, pad):
            return lax.conv_general_dilated(h, w, window_strides=(1,), padding=[(pad, pad)], dimension_numbers=('NCH', 'OIH', 'NCH'))
        d = x.shape[-1]
        xc = jnp.transpose(x, (0, 2, 1))
        h = _bn(_conv1d(xc, conv1_w, 0), bn1_g, bn1_b, bn1_m, bn1_v)
        h = jax.nn.relu(h)
        h = _bn(_conv1d(h, conv2_w, 8), bn2_g, bn2_b, bn2_m, bn2_v)
        x_conv = jnp.transpose(jax.nn.relu(h + xc), (0, 2, 1))
        s = x @ w_se.T + b_se
        sq = jnp.sum(s * s, axis=-1)
        dist = sq[:, :, None] + sq[:, None, :] - 2.0 * jnp.einsum('bnd,bmd->bnm', s, s)
        A = jnp.exp(-dist) * mask
        msg = jax.nn.relu(x @ w_msg.T + b_msg)
        x_nmp = jnp.einsum('bnm,bmd->bnd', A, msg)
        x_in = jnp.concatenate([x_conv, x_nmp], axis=-1)
        gi = x_in @ w_ih.T + b_ih
        gh = x @ w_hh.T + b_hh
        gi_r, gi_z, gi_n = (gi[..., :d], gi[..., d:2 * d], gi[..., 2 * d:])
        gh_r, gh_z, gh_n = (gh[..., :d], gh[..., d:2 * d], gh[..., 2 * d:])
        r = jax.nn.sigmoid(gi_r + gh_r)
        z = jax.nn.sigmoid(gi_z + gh_z)
        nn_ = jnp.tanh(gi_n + r * gh_n)
        return (1.0 - z) * nn_ + z * x

    def _L0_ffn_ref(x, Wg, bg, W1, b1, W2, b2):
        import jax, jax.numpy as jnp
        import numpy as np
        B, S, D, E, H, K = (4, 2048, 128, 8, 256, 2)
        Bv, Sv, Dv = x.shape
        gate_scores = x @ Wg + bg
        _, idx = jax.lax.top_k(gate_scores, K)
        mask = jax.nn.one_hot(idx, E, dtype=x.dtype).sum(axis=-2)
        xf = x.reshape(-1, Dv)
        mf = mask.reshape(-1, E)
        h = jax.nn.gelu(jnp.einsum('td,edh->teh', xf, W1) + b1[None], approximate=False)
        y = jnp.einsum('teh,ehd->ted', h, W2) + b2[None]
        out = jnp.einsum('ted,te->td', y, mf)
        return out.reshape(Bv, Sv, Dv)
    x = x + _L0_gnn_ref(_layernorm(x, axis=-1), adj, L0_gnn_w_se, L0_gnn_b_se, L0_gnn_conv1_w, L0_gnn_bn1_g, L0_gnn_bn1_b, L0_gnn_bn1_m, L0_gnn_bn1_v, L0_gnn_conv2_w, L0_gnn_bn2_g, L0_gnn_bn2_b, L0_gnn_bn2_m, L0_gnn_bn2_v, L0_gnn_w_msg, L0_gnn_b_msg, L0_gnn_w_ih, L0_gnn_b_ih, L0_gnn_w_hh, L0_gnn_b_hh)
    x = x + _L0_ffn_ref(_layernorm(x, axis=-1), L0_ffn_Wg, L0_ffn_bg, L0_ffn_W1, L0_ffn_b1, L0_ffn_W2, L0_ffn_b2)
    return x

_drawn_inputs = setup_inputs


def setup_inputs(seed=0):
    import zlib

    import numpy as np

    out = dict(_drawn_inputs(seed))
    spreads = {'L0_gnn_b_se': (0.0, 0.8),
     'L0_gnn_bn1_g': (1.0, 0.6),
     'L0_gnn_bn1_b': (0.0, 0.418),
     'L0_gnn_bn1_m': (0.0, 0.387),
     'L0_gnn_bn1_v': (1.0, 0.6),
     'L0_gnn_bn2_g': (1.0, 0.6),
     'L0_gnn_bn2_b': (0.0, 0.584),
     'L0_gnn_bn2_m': (0.0, 0.564),
     'L0_gnn_bn2_v': (1.0, 0.6),
     'L0_gnn_b_msg': (0.0, 0.1),
     'L0_gnn_b_ih': (0.0, 0.1),
     'L0_gnn_b_hh': (0.0, 0.296),
     'L0_ffn_bg': (0.0, 0.1),
     'L0_ffn_b1': (0.0, 0.544),
     'L0_ffn_b2': (0.0, 0.1)}
    factors = {}
    for name, (base, spread) in spreads.items():
        noise = np.random.default_rng([zlib.crc32(name.encode()), seed]).standard_normal(out[name].shape)
        drawn = base * np.exp(spread * noise) if base else spread * noise
        out[name] = jnp.asarray(drawn.astype(out[name].dtype))
    for name, factor in factors.items():
        out[name] = (out[name] * factor).astype(out[name].dtype)
    return out
```

```python
from contextlib import ExitStack

import concourse.bass as bass
from concourse import mybir

F32 = mybir.dt.float32
F32R = mybir.dt.float32r
BF16 = mybir.dt.bfloat16
ALU = mybir.AluOpType
ACT = mybir.ActivationFunctionType
AX = mybir.AxisListType

P = 128
GRAPHS, NODES, D = 32, 256, 128
GP = 2
BLOCK = GP * NODES
TILES = BLOCK // P
MB = NODES // P
BLOCKS = GRAPHS // GP
TAPS, PAD = 17, 8
WIDE = NODES + 2 * PAD
EXPERTS, HID = 8, 256
CH = HID // P
EPS = 1e-5
SE = 96

(BN1_G, BN1_B, BN1_M, BN1_V, BN2_G, BN2_B, BN2_M, BN2_V, BIH_R, BIH_Z, BIH_N, BHH_R, BHH_Z, BHH_N,
 BSE) = range(15)
B1_AT = 15
B2_AT = B1_AT + EXPERTS * CH
NVEC = B2_AT + EXPERTS


class Block:

    def __init__(self, k, off):
        self.k, self.off = k, off

    def __add__(self, n):
        return Block(self.k, self.off + n)

    @property
    def index(self):
        return 2 * self.k + self.off

    @property
    def par(self):
        return self.off % 2

    @property
    def half(self):
        return self.k + self.off // 2

    def known(self, low, high):
        return not isinstance(self.k, int) or low <= self.index < high


def build(nc, a, out):
    ctx = ExitStack()
    with ctx:
        def sb(name, shape, dt=F32):
            return ctx.enter_context(nc.sbuf_tensor(name, shape, dt))

        def sem(name):
            return ctx.enter_context(nc.semaphore(name))

        w2c_hi = sb("w2c_hi", [P, TAPS, D], F32R)
        w2c_lo = sb("w2c_lo", [P, TAPS, D], F32R)
        w1c_hi = sb("w1c_hi", [P, D], F32R)
        w1c_lo = sb("w1c_lo", [P, D], F32R)
        wse_hi = sb("wse_hi", [P, SE], F32R)
        wse_lo = sb("wse_lo", [P, SE], F32R)
        wg_hi = sb("wgru_hi", [P, 3, 3 * D], F32R)
        wg_lo = sb("wgru_lo", [P, 3, 3 * D], F32R)
        wmsg = sb("wmsg", [P, D])
        wgate = sb("wgate", [P, P])
        wu_hi = sb("wup_hi", [P, EXPERTS, HID], F32R)
        wu_lo = sb("wup_lo", [P, EXPERTS, HID], F32R)
        wd_hi = sb("wdown_hi", [P, EXPERTS, CH, D], F32R)
        wd_lo = sb("wdown_lo", [P, EXPERTS, CH, D], F32R)
        vec = sb("vec", [P, NVEC])
        bmsg = sb("bmsg", [P, TILES * D])
        bgate = sb("bgate", [P, TILES * EXPERTS])
        ident = sb("ident", [P, P])
        identb = sb("identb", [P, P], BF16)
        earlier = sb("earlier", [P, EXPERTS, EXPERTS])
        ones8 = sb("halfpow", [P, 8])
        bnv = sb("bnv", [P, 2])
        bnr = sb("bnr", [P, 2])
        bnt = sb("bnt", [P, 2])
        spare = sb("spare", [P, 1])
        s1 = sb("s1", [P, 1])
        o1 = sb("o1", [P, 1])
        s2 = sb("s2", [P, 1])
        o2 = sb("o2", [P, 1])
        hb = sb("hb", [P, 3])
        STAGE = TAPS * D + 2 * EXPERTS * HID + 9 * D + D + SE
        stage = sb("stage", [P, STAGE])
        at = [0]

        def view(n, dt=F32):
            lo = at[0]
            at[0] += n
            v = stage[:, lo:lo + n]
            return v if dt is F32 else v.bitcast(dt)

        raw_w2c = view(TAPS * D)
        raw_w1c = view(D)
        raw_wse = view(SE)
        raw_wg = view(9 * D)
        raw_wu = view(EXPERTS * HID)
        raw_wd = view(EXPERTS * HID)
        at[0] = 0
        maskb = [view(EXPERTS * BLOCK // 2, BF16).rearrange("p (e t) -> p e t", e=EXPERTS)
                 for _ in range(2)]
        y2x = [view(BLOCK) for _ in range(2)]
        x1r = [view(BLOCK) for _ in range(2)]
        ym = [view(BLOCK) for _ in range(2)]
        assert at[0] <= STAGE

        xt = sb("xtok", [P, 2, TILES, D])
        adj = sb("adj", [P, 2, TILES, NODES])
        xT = sb("xT", [P, 2, BLOCK])
        st = sb("st", [P, TILES, 6])
        mv = sb("mv", [P, TILES, 2])
        ve = sb("ve", [P, TILES])
        rs = sb("rs", [P, TILES])
        st2 = sb("st2", [P, TILES, 6])
        mv2 = sb("mv2", [P, TILES, 2])
        ve2 = sb("ve2", [P, TILES])
        rs2 = sb("rs2", [P, TILES])
        xn = sb("xn", [P, TILES, D])
        xnf = sb("xnT", [P, 2, BLOCK])
        xnh = sb("xnT_hi", [P, 2, BLOCK], F32R)
        xnl = sb("xnT_lo", [P, 2, BLOCK], F32R)
        h1f = sb("h1", [P, GP, NODES])
        h1h = sb("h1_hi", [P, 2, GP, WIDE], F32R)
        h1l = sb("h1_lo", [P, 2, GP, WIDE], F32R)
        L = sb("L", [SE, BLOCK])
        R = sb("R", [SE, BLOCK])
        am = sb("am", [P, TILES, NODES])
        ah = sb("a_hi", [P, TILES, NODES], F32R)
        al = sb("a_lo", [P, TILES, NODES], F32R)
        mt = sb("mt", [P, TILES * D])
        mf = sb("msg", [P, TILES * D])
        mh = sb("msg_hi", [P, BLOCK], F32R)
        ml = sb("msg_lo", [P, BLOCK], F32R)
        nh = sb("nmp_hi", [P, BLOCK], F32R)
        nl = sb("nmp_lo", [P, BLOCK], F32R)
        ct = sb("ct", [P, BLOCK])
        cf = sb("xconv", [P, BLOCK])
        chh = sb("xconv_hi", [P, BLOCK], F32R)
        cl = sb("xconv_lo", [P, BLOCK], F32R)
        rt = sb("rt", [P, BLOCK])
        zt = sb("zt", [P, BLOCK])
        uu = sb("uu", [P, BLOCK])
        vv = sb("vv", [P, BLOCK])
        nn = sb("nn", [P, BLOCK])
        dd = sb("dd", [P, BLOCK])
        x1 = sb("x1T", [P, BLOCK])
        xn2 = sb("xn2", [P, TILES, D])
        x2c = sb("xn2T", [P, BLOCK])
        gs = sb("gs", [P, TILES, EXPERTS])
        cmp_ = sb("cmp", [P, TILES, EXPERTS, EXPERTS])
        ceq = sb("ceq", [P, TILES, EXPERTS, EXPERTS])
        rank = sb("rank", [P, TILES, EXPERTS])
        mask = sb("mask", [P, TILES * EXPERTS], BF16)
        maskT = sb("maskT", [TILES * EXPERTS, P], BF16)

        hf = [am[:, :, :].rearrange("p t n -> p (t n)"),
              xnf[:, :, :].rearrange("p t n -> p (t n)")]
        hh = [ah[:, :, :].rearrange("p t n -> p (t n)"), al[:, :, :].rearrange("p t n -> p (t n)")]
        hl = [xnh[:, :, :].rearrange("p t n -> p (t n)"), xnl[:, :, :].rearrange("p t n -> p (t n)")]
        qh = [mh[:, :], nh[:, :]]
        ql = [ml[:, :], nl[:, :]]

        banks = [ctx.enter_context(nc.psum_tensor(f"bank{n}", [P, BLOCK], F32)) for n in range(8)]
        X0, X1, X2, C2, PR, PZ, PI, PH = banks
        up = [[PR, PZ], [PI, PH]]
        down = [C2, X0]

        d_x1 = nc.dram_tensor("kept_x1", [P, GRAPHS * NODES], F32, kind="Internal").ap()
        d_x2 = nc.dram_tensor("kept_xn2", [P, GRAPHS * NODES], F32, kind="Internal").ap()
        d_mk = nc.dram_tensor("kept_mask", [EXPERTS, GRAPHS * NODES], BF16, kind="Internal").ap()

        def f32(ap):
            return ap.bitcast(F32)

        names = """ld_x0 ld_x1 ld_adj0 ld_adj1 ld_t0 ld_t1 ld_w2c ld_w1 ld_g ld_ff ld_c ld_c2 st_x1 st_x2
            st_mk k_init k_sp_dve k_w1 k_g k_ff_hi k_ff k_bn k_bnp k_bnr k_bno k_hb k_id k_ones
            v_st v_agg v_var v_norm p_rs v_rs2 p_rs2 v_st2 v_agg2
            t_in t_conv1 t_s t_msg t_dist0 t_dist1 t_av t_x1 t_x2 t_conv2 t_gate t_gh t_r t_z t_n
            t_mask a_xnh a_xnf a_h1 a_h1h a_sq0 a_sq1 a_msg a_msgh a_e0 a_e1 a_ah a_nh a_c a_ch a_rt
            a_zt a_u a_nn a_x2 v_xnl v_h1l v_r0 v_l0 v_mt v_ml v_am v_al v_nl v_ct v_cl v_v v_w v_d
            v_e v_g v_x1 v_norm2 v_gs v_cmp v_ceq v_sum v_rank v_mask v_mT
            f_mk0 f_mk1 f_x20 f_x21 f_x10 f_x11 f_qh f_ql f_up f_h f_hh f_hl f_down f_ym f_acc
            f_out f_ff""".split()
        s = {n: sem(n) for n in names}

        def after(e, name, b):
            if b.known(0, BLOCKS):
                e.wait_ge(s[name], b.index + 1)

        def loaded(e, name, b):
            e.wait_ge(s[f"{name}{b.par}"], 16 * (b.half + 1))

        def tok(ap, b):
            return ap[:, bass.ds(b.index * BLOCK, BLOCK)]

        x_d = a["x"].rearrange("(b j p) d -> b p j d", j=TILES, p=P)
        adj_d = a["adjT"].rearrange("(b j p) n -> b p j n", j=TILES, p=P)

        ctx2 = ctx.enter_context(nc.Block())
        blk = ctx2

        def pairs_loop(e, first, rounds, body):
            with e.Fori(0, rounds) as k:
                body(Block(k, first))
                body(Block(k, first + 1))

        @blk.sync
        def _(e):
            def load_x(b):
                after(e, "v_norm", b + -2)
                e.dma_start(xt[:, b.par], x_d[b.index]).then_inc(s[f"ld_x{b.par}"], 16)

            def load_adj(b):
                after(e, "v_am", b + -2)
                e.dma_start(adj[:, b.par], adj_d[b.index]).then_inc(s[f"ld_adj{b.par}"], 16)

            def load_xT(b):
                after(e, "v_x1", b + -2)
                e.dma_start(xT[:, b.par], tok(a["xT"], b)).then_inc(s[f"ld_t{b.par}"], 16)

            def keep_x1(b):
                after(e, "v_x1", b)
                e.dma_start(tok(d_x1, b), x1[:, :]).then_inc(s["st_x1"], 16)

            def store_mask(b):
                e.dma_start(tok(d_mk, b).rearrange("e (j t) -> j e t", j=TILES),
                            maskT[:, :]).then_inc(s["st_mk"], 16)

            def keep_x2(b):
                after(e, "v_mT", b + -1)
                after(e, "a_x2", b)
                e.dma_start(tok(d_x2, b), x2c[:, :]).then_inc(s["st_x2"], 16)
                if b.known(1, BLOCKS):
                    store_mask(b + -1)

            def body(b):
                if b.known(0, BLOCKS - 2):
                    load_x(b + 2)
                    load_adj(b + 2)
                if b.known(1, BLOCKS):
                    keep_x1(b + -1)
                if b.known(0, BLOCKS - 1):
                    load_xT(b + 1)
                if b.known(1, BLOCKS):
                    keep_x2(b + -1)

            load_x(Block(0, 0))
            e.dma_start(ident[:, :], a["ident"]).then_inc(s["ld_c"], 16)
            e.dma_start(raw_w1c, a["conv1"]).then_inc(s["ld_w1"], 16)
            e.dma_start(raw_wse, a["wse"]).then_inc(s["ld_w1"], 16)
            e.dma_start(vec[:, :], a["vec"]).then_inc(s["ld_c"], 16)
            e.dma_start(wmsg[:, :], a["wmsg"]).then_inc(s["ld_c"], 16)
            e.dma_start(bmsg[:, :], a["bmsg"]).then_inc(s["ld_c"], 16)
            load_adj(Block(0, 0))
            e.dma_start(raw_w2c, a["conv2"]).then_inc(s["ld_w2c"], 16)
            load_x(Block(0, 1))
            e.dma_start(raw_wg, a["wgru"]).then_inc(s["ld_g"], 16)
            load_xT(Block(0, 0))
            load_adj(Block(0, 1))
            e.dma_start(wgate[:, :], a["wgate"]).then_inc(s["ld_c2"], 16)
            e.dma_start(bgate[:, :], a["bgate"]).then_inc(s["ld_c2"], 16)
            e.dma_start(earlier[:, :, :], a["earlier"]).then_inc(s["ld_c2"], 16)
            e.dma_start(raw_wu, a["wup"]).then_inc(s["ld_ff"], 16)
            e.dma_start(raw_wd, a["wdown"]).then_inc(s["ld_ff"], 16)
            def fetch(b):
                e.wait_ge(s["st_x1"], 16 * (b.index + 1))
                e.wait_ge(s["st_x2"], 16 * (b.index + 1))
                e.wait_ge(s["st_mk"], 16 * (b.index + 1))
                if b.known(2, BLOCKS):
                    e.wait_ge(s["f_ql"], b.index - 1)
                    e.wait_ge(s["f_qh"], b.index - 1)
                e.dma_start(y2x[b.par], tok(d_x2, b)).then_inc(s[f"f_x2{b.par}"], 16)
                e.dma_start(maskb[b.par], tok(d_mk, b).unsqueeze(0).broadcast_to([P, EXPERTS, BLOCK])
                            ).then_inc(s[f"f_mk{b.par}"], 16)
                if b.known(2, BLOCKS):
                    e.wait_ge(s["f_out"], 16 * (b.index - 1))
                e.dma_start(x1r[b.par], tok(d_x1, b)).then_inc(s[f"f_x1{b.par}"], 16)

            def store(b):
                e.wait_ge(s["f_acc"], EXPERTS * (b.index + 1))
                e.dma_start(tok(out, b), x1r[b.par]).then_inc(s["f_out"], 16)

            def turn(b):
                store(b)
                if b.known(0, BLOCKS - 2):
                    fetch(b + 2)

            body(Block(0, 0))
            body(Block(0, 1))
            pairs_loop(e, 2, (BLOCKS - 4) // 2, body)
            e.wait_ge(s["k_ff"], 4)
            e.wait_ge(s["k_sp_dve"], 4)
            fetch(Block(0, 0))
            fetch(Block(0, 1))
            body(Block(0, BLOCKS - 2))
            body(Block(0, BLOCKS - 1))
            last = Block(0, BLOCKS - 1)
            keep_x1(last)
            keep_x2(last)
            after(e, "v_mT", last)
            store_mask(last)
            pairs_loop(e, 0, (BLOCKS - 2) // 2, turn)
            turn(Block(0, BLOCKS - 2))
            turn(Block(0, BLOCKS - 1))
            e.wait_ge(s["f_out"], 16 * BLOCKS)

        @blk.gpsimd
        def _(e):
            e.memset(ones8[:, :], -0.5).then_inc(s["k_init"], 1)
            e.memset(h1h[:, :, :, :].bitcast(F32), 0.0).then_inc(s["k_init"], 1)
            e.memset(h1l[:, :, :, :].bitcast(F32), 0.0).then_inc(s["k_init"], 1)
            e.wait_ge(s["k_init"], 3)
            e.wait_ge(s["k_bn"], 2)
            e.tensor_tensor(bnr[:, :], bnv[:, :], ones8[:, 0:2], ALU.pow).then_inc(s["k_bnp"], 1)

            def root(b):
                after(e, "v_var", b)
                after(e, "v_norm", b + -1)
                e.tensor_tensor(rs[:, :], ve[:, :], ones8[:, 0:TILES], ALU.pow).then_inc(s["p_rs"], 1)

            def root2(b):
                after(e, "v_rs2", b)
                after(e, "v_norm2", b + -1)
                e.tensor_tensor(rs2[:, :], ve2[:, :], ones8[:, 0:TILES], ALU.pow).then_inc(s["p_rs2"], 1)

            def body(b):
                first = isinstance(b.k, int) and b.index < PIECES
                if b.known(0, BLOCKS - 1):
                    root(b + 1)
                if first:
                    split_piece(b.index)
                if b.known(1, BLOCKS + 1):
                    root2(b + -1)

            flat = [t[:, :, :].rearrange("p e n -> p (e n)") for t in (wu_hi, wu_lo)] + \
                   [t[:, :, :, :].rearrange("p e c n -> p (e c n)") for t in (wd_hi, wd_lo)]
            PIECES = 2
            width = EXPERTS * HID // PIECES

            def split_piece(i):
                if i == 0:
                    e.wait_ge(s["ld_ff"], 32)
                for m, raw in enumerate((raw_wu, raw_wd)):
                    part = slice(i * width, (i + 1) * width)
                    e.tensor_copy(flat[2 * m][:, part], raw[:, part]).then_inc(s["k_ff_hi"], 1)
                    e.wait_ge(s["k_ff_hi"], 2 * i + m + 1)
                    e.tensor_tensor(flat[2 * m + 1][:, part], raw[:, part], f32(flat[2 * m][:, part]),
                                    ALU.subtract).then_inc(s["k_ff"], 1)

            root(Block(0, 0))
            for n in range(3):
                body(Block(0, n))
            pairs_loop(e, 3, (BLOCKS - 4) // 2, body)
            body(Block(0, BLOCKS - 1))
            root2(Block(0, BLOCKS - 1))

        def f_split_waits(e, b):
            if b.known(2, BLOCKS):
                e.wait_ge(s["f_up"], CH * EXPERTS * (b.index - 1))
            loaded(e, "f_x2", b)

        @blk.scalar
        def _(e):
            def act(o, i, f, sig, **kw):
                return e.activation(o, i, f, **kw).then_inc(s[sig], 1)

            e.wait_ge(s["ld_w1"], 32)
            act(w1c_hi[:, :], raw_w1c, ACT.Copy, "k_w1")
            act(wse_hi[:, :], raw_wse, ACT.Copy, "k_w1")

            def gru(b):
                after(e, "t_gh", b)
                after(e, "v_v", b + -1)
                act(uu[:, :], PH[:, :], ACT.Identity, "a_u", scale=0.5, bias=hb[:, 2:3])
                after(e, "t_r", b)
                act(rt[:, :], PR[:, :], ACT.Tanh, "a_rt", scale=0.5, bias=hb[:, 0:1])
                after(e, "t_z", b)
                after(e, "v_e", b + -1)
                act(zt[:, :], PZ[:, :], ACT.Tanh, "a_zt", scale=0.5, bias=hb[:, 1:2])
                after(e, "v_w", b)
                after(e, "v_g", b + -1)
                act(nn[:, :], vv[:, :], ACT.Tanh, "a_nn", bias=vec[:, BIH_N:BIH_N + 1])

            def nmp_hi(b):
                after(e, "t_av", b)
                after(e, "t_n", b + -1)
                act(nh[:, :], PH[:, :], ACT.Copy, "a_nh")

            def norm_out(b):
                after(e, "t_in", b)
                after(e, "t_n", b + -2)
                after(e, "v_d", b + -2)
                act(xnh[:, b.par], X0[:, :], ACT.Copy, "a_xnh")
                act(xnf[:, b.par], X0[:, :], ACT.Copy, "a_xnf")

            def conv1_out(b):
                after(e, "t_conv1", b)
                if isinstance(b.k, int) and b.index == 0:
                    e.wait_ge(s["k_bno"], 2)
                    e.wait_ge(s["k_init"], 3)
                kw = dict(scale=s1[:, 0:1], bias=o1[:, 0:1])
                ps = X1[:, :].rearrange("p (g n) -> p g n", g=GP)
                after(e, "t_conv2", b + -2)
                act(h1h[:, b.par, :, PAD:PAD + NODES], ps, ACT.Relu, "a_h1h", **kw)
                after(e, "v_h1l", b + -1)
                act(h1f[:, :, :], ps, ACT.Relu, "a_h1", **kw)

            def squares(b):
                if isinstance(b.k, int) and b.index == 0:
                    e.wait_ge(s["ld_c"], 64)
                after(e, "t_s", b)
                after(e, "t_dist1", b + -1)
                act(R[32:64, :], X2[32:64, :], ACT.Square, "a_sq0", bias=vec[32:64, BSE:BSE + 1])
                act(L[64:96, :], X2[64:96, :], ACT.Square, "a_sq1", bias=vec[64:96, BSE:BSE + 1])

            def messages(b):
                after(e, "v_mt", b)
                after(e, "t_av", b + -1)
                act(mh[:, :], mt[:, :], ACT.Relu, "a_msgh")
                after(e, "v_ml", b + -1)
                act(mf[:, :], mt[:, :], ACT.Relu, "a_msg")

            def weights_of(b):
                after(e, "v_al", b + -1)
                after(e, "a_ah", b + -1)
                for g, ps in enumerate((PZ, PI)):
                    after(e, f"t_dist{g}", b)
                    act(am[:, g * MB:(g + 1) * MB, :], ps[:, :].rearrange("p (m n) -> p m n", m=MB),
                        ACT.Exp, f"a_e{g}", scale=-1.0)

            def weights_hi(b):
                after(e, "v_am", b)
                after(e, "t_av", b + -1)
                act(ah[:, :, :], am[:, :, :], ACT.Copy, "a_ah")

            def norm2_out(b):
                after(e, "t_x2", b)
                after(e, "t_gate", b + -1)
                if b.known(1, BLOCKS):
                    e.wait_ge(s["st_x2"], 16 * b.index)
                act(x2c[:, :], X1[:, :], ACT.Copy, "a_x2")

            def conv2_out(b):
                after(e, "v_ct", b)
                after(e, "t_n", b + -1)
                act(chh[:, :], ct[:, :], ACT.Relu, "a_ch", bias=o2[:, 0:1])
                after(e, "v_cl", b + -1)
                act(cf[:, :], ct[:, :], ACT.Relu, "a_c", bias=o2[:, 0:1])

            def body(b):
                prev, nxt = b.known(1, BLOCKS + 1), b.known(0, BLOCKS - 1)
                if prev:
                    gru(b + -1)
                nmp_hi(b)
                if nxt:
                    norm_out(b + 1)
                    squares(b + 1)
                    conv1_out(b + 1)
                    messages(b + 1)
                    weights_of(b + 1)
                    weights_hi(b + 1)
                conv2_out(b)
                if prev:
                    norm2_out(b + -1)

            norm_out(Block(0, 0))
            e.wait_ge(s["ld_w2c"], 16)
            act(w2c_hi[:, :, :].rearrange("p k n -> p (k n)"), raw_w2c, ACT.Copy, "k_g")
            squares(Block(0, 0))
            conv1_out(Block(0, 0))
            messages(Block(0, 0))
            weights_of(Block(0, 0))
            weights_hi(Block(0, 0))
            e.wait_ge(s["ld_g"], 16)
            act(wg_hi[:, :, :].rearrange("p k n -> p (k n)"), raw_wg, ACT.Copy, "k_g")
            for n in range(3):
                body(Block(0, n))
            pairs_loop(e, 3, (BLOCKS - 4) // 2, body)
            body(Block(0, BLOCKS - 1))

            def split(b):
                f_split_waits(e, b)
                act(qh[b.par], y2x[b.par], ACT.Copy, "f_qh")

            def hidden(b, x):
                p, n = x % 2, EXPERTS * b.index + x
                old = x >= 2 or b.known(1, BLOCKS)
                for c in range(CH):
                    part = slice(c * BLOCK, (c + 1) * BLOCK)
                    e.wait_ge(s["f_up"], CH * n + c + 1)
                    if old and c == 0:
                        e.wait_ge(s["f_hl"], CH * (n - 1))
                    act(hf[p][:, part], up[p][c][:, :], ACT.Gelu, "f_h",
                        bias=vec[:, B1_AT + x * CH + c:B1_AT + x * CH + c + 1])
                    e.wait_ge(s["f_h"], CH * n + c + 1)
                    if old and c == 0:
                        e.wait_ge(s["f_down"], n - 1)
                    act(hh[p][:, part], hf[p][:, part], ACT.Copy, "f_hh")

            def turn(b):
                for x in range(EXPERTS):
                    if isinstance(b.k, int) and b.index == 0 and x == 2:
                        norm2_out(Block(0, BLOCKS - 1))
                    if x == EXPERTS - 2 and b.known(0, BLOCKS - 1):
                        split(b + 1)
                    hidden(b, x)

            last = Block(0, BLOCKS - 1)
            after(e, "t_av", last)
            split(Block(0, 0))
            gru(last)
            after(e, "v_d", last)
            turn(Block(0, 0))
            pairs_loop(e, 1, (BLOCKS - 2) // 2, turn)
            turn(Block(0, BLOCKS - 1))

        @blk.vector
        def _(e):
            def tt(o, i, j, op, sig):
                return e.tensor_tensor(o, i, j, op).then_inc(s[sig], 1)

            e.memset(R[64:96, :], 1.0).then_inc(s["k_ones"], 1)
            e.memset(L[32:64, :], 1.0).then_inc(s["k_ones"], 1)
            e.wait_ge(s["ld_c"], 64)
            e.tensor_scalar(bnv[:, 0:1], vec[:, BN1_V:BN1_V + 1], EPS, None, ALU.add).then_inc(s["k_bn"], 1)
            e.tensor_scalar(bnv[:, 1:2], vec[:, BN2_V:BN2_V + 1], EPS, None, ALU.add).then_inc(s["k_bn"], 1)
            for n, at_b in enumerate((BHH_R, BHH_Z)):
                tt(hb[:, n:n + 1], vec[:, BIH_R + n:BIH_R + n + 1], vec[:, at_b:at_b + 1], ALU.add, "k_hb")
            e.tensor_copy(hb[:, 2:3], vec[:, BHH_N:BHH_N + 1]).then_inc(s["k_hb"], 1)
            e.tensor_copy(identb[:, :], ident[:, :]).then_inc(s["k_id"], 1)
            e.wait_ge(s["k_hb"], 3)
            e.tensor_scalar(hb[:, :], hb[:, :], 0.5, None, ALU.mult).then_inc(s["k_hb"], 1)

            def settled(e, name, b):
                after(e, name, b)
                e.memset(spare[:, :], 0.0)

            def stats(b):
                loaded(e, "ld_x", b)
                after(e, "v_agg", b + -1)
                for j in range(TILES):
                    q = e.bn_stats(st[:, j, :], xt[:, b.par, j, :])
                q.then_inc(s["v_st"], 1)
                settled(e, "v_st", b)
                for j in range(TILES):
                    q = e.bn_aggr(mv[:, j, :], st[:, j, :])
                q.then_inc(s["v_agg"], 1)
                after(e, "v_agg", b)
                after(e, "p_rs", b + -1)
                e.tensor_scalar(ve[:, :], mv[:, :, 1], EPS, None, ALU.add).then_inc(s["v_var"], 1)

            def normalize(b):
                after(e, "p_rs", b)
                after(e, "t_in", b + -1)
                for j in range(TILES):
                    q = e.tensor_scalar(xn[:, j, :], xt[:, b.par, j, :], mv[:, j, 0:1],
                                        rs[:, j:j + 1], ALU.subtract, ALU.mult)
                q.then_inc(s["v_norm"], 1)

            def gru_a(b):
                after(e, "a_u", b)
                after(e, "a_rt", b)
                after(e, "a_nn", b + -1)
                e.scalar_tensor_tensor(out=vv[:, :], in0=rt[:, :], scalar=1.0, in1=uu[:, :],
                                       op0=ALU.add, op1=ALU.mult).then_inc(s["v_v"], 1)
                after(e, "v_v", b)
                after(e, "t_n", b)
                tt(vv[:, :], PI[:, :], vv[:, :], ALU.add, "v_w")

            def gru_d(b):
                after(e, "a_nn", b)
                tt(dd[:, :], xnf[:, b.par], nn[:, :], ALU.subtract, "v_d")

            def gru_b(b):
                after(e, "v_d", b)
                after(e, "a_zt", b)
                e.scalar_tensor_tensor(out=dd[:, :], in0=zt[:, :], scalar=1.0, in1=dd[:, :],
                                       op0=ALU.add, op1=ALU.mult).then_inc(s["v_e"], 1)
                after(e, "v_e", b)
                e.scalar_tensor_tensor(out=dd[:, :], in0=dd[:, :], scalar=0.5, in1=nn[:, :],
                                       op0=ALU.mult, op1=ALU.add).then_inc(s["v_g"], 1)
                after(e, "v_g", b)
                loaded(e, "ld_t", b)
                after(e, "t_x1", b + -1)
                if b.known(1, BLOCKS):
                    e.wait_ge(s["st_x1"], 16 * b.index)
                tt(x1[:, :], dd[:, :], xT[:, b.par], ALU.add, "v_x1")

            def nmp_lo(b):
                after(e, "a_nh", b)
                after(e, "t_n", b + -1)
                tt(nl[:, :], PH[:, :], f32(nh[:, :]), ALU.subtract, "v_nl")

            def norm_lo(b):
                after(e, "a_xnh", b)
                after(e, "a_xnf", b)
                after(e, "t_n", b + -2)
                tt(xnl[:, b.par], X0[:, :], f32(xnh[:, b.par]), ALU.subtract, "v_xnl")

            def conv1_lo(b):
                after(e, "a_h1", b)
                after(e, "a_h1h", b)
                after(e, "t_conv2", b + -2)
                tt(h1l[:, b.par, :, PAD:PAD + NODES], h1f[:, :, :],
                   f32(h1h[:, b.par, :, PAD:PAD + NODES]), ALU.subtract, "v_h1l")

            def embed(b):
                after(e, "a_sq1", b)
                after(e, "t_dist1", b + -1)
                e.tensor_scalar(R[0:32, :], X2[0:32, :], vec[0:32, BSE:BSE + 1], None,
                                ALU.add).then_inc(s["v_r0"], 1)
                e.tensor_scalar(L[0:32, :], X2[0:32, :], vec[0:32, BSE:BSE + 1], -2.0,
                                ALU.add, ALU.mult).then_inc(s["v_l0"], 1)

            def messages(b):
                after(e, "t_msg", b)
                after(e, "a_msg", b + -1)
                tt(mt[:, :], PR[:, :], bmsg[:, :], ALU.add, "v_mt")

            def messages_lo(b):
                after(e, "a_msg", b)
                after(e, "t_av", b + -1)
                tt(ml[:, :], mf[:, :], f32(mh[:, :]), ALU.subtract, "v_ml")

            def weights(b):
                after(e, "a_e1", b)
                loaded(e, "ld_adj", b)
                tt(am[:, :, :], am[:, :, :], adj[:, b.par], ALU.mult, "v_am")

            def weights_lo(b):
                after(e, "a_ah", b)
                after(e, "t_av", b + -1)
                tt(al[:, :, :], am[:, :, :], f32(ah[:, :, :]), ALU.subtract, "v_al")

            def stats2(b):
                after(e, "t_x1", b)
                for j in range(TILES):
                    q = e.bn_stats(st2[:, j, :], X0[:, j * P:(j + 1) * P])
                q.then_inc(s["v_st2"], 1)
                settled(e, "v_st2", b)
                for j in range(TILES):
                    q = e.bn_aggr(mv2[:, j, :], st2[:, j, :])
                q.then_inc(s["v_agg2"], 1)
                after(e, "v_agg2", b)
                after(e, "p_rs2", b + -1)
                e.tensor_scalar(ve2[:, :], mv2[:, :, 1], EPS, None, ALU.add).then_inc(s["v_rs2"], 1)

            def normalize2(b):
                after(e, "p_rs2", b)
                after(e, "t_x2", b + -1)
                for j in range(TILES):
                    q = e.tensor_scalar(xn2[:, j, :], X0[:, j * P:(j + 1) * P], mv2[:, j, 0:1],
                                        rs2[:, j:j + 1], ALU.subtract, ALU.mult)
                q.then_inc(s["v_norm2"], 1)

            def conv2_sum(b):
                after(e, "t_conv2", b)
                after(e, "a_c", b + -1)
                e.scalar_tensor_tensor(out=ct[:, :], in0=C2[:, :], scalar=s2[:, 0:1],
                                       in1=xnf[:, b.par], op0=ALU.mult, op1=ALU.add
                                       ).then_inc(s["v_ct"], 1)

            def conv2_lo(b):
                after(e, "a_c", b)
                after(e, "t_n", b + -1)
                tt(cl[:, :], cf[:, :], f32(chh[:, :]), ALU.subtract, "v_cl")

            def choose(b):
                after(e, "t_gate", b)
                sc = X2[:, :].rearrange("p (j n) -> p j n", j=TILES)[:, :, 0:EXPERTS]
                tt(gs[:, :, :], sc, bgate[:, :].rearrange("p (j n) -> p j n", j=TILES), ALU.add, "v_gs")

            def choose_b(b):
                after(e, "v_gs", b)
                shape = [P, TILES, EXPERTS, EXPERTS]
                other = gs[:, :, :].unsqueeze(2).broadcast_to(shape)
                own = gs[:, :, :].unsqueeze(3).broadcast_to(shape)
                tt(cmp_[:, :, :, :], other, own, ALU.is_gt, "v_cmp")
                tt(ceq[:, :, :, :], other, own, ALU.is_equal, "v_ceq")
                after(e, "v_ceq", b)
                tt(ceq[:, :, :, :], ceq[:, :, :, :],
                   earlier[:, :, :].unsqueeze(1).broadcast_to(shape), ALU.mult, "v_sum")
                e.wait_ge(s["v_sum"], 2 * b.index + 1)
                after(e, "v_cmp", b)
                tt(cmp_[:, :, :, :], cmp_[:, :, :, :], ceq[:, :, :, :], ALU.add, "v_sum")
                e.wait_ge(s["v_sum"], 2 * b.index + 2)
                e.tensor_reduce(rank[:, :, :], cmp_[:, :, :, :], AX.X, ALU.add).then_inc(s["v_rank"], 1)
                after(e, "v_rank", b)
                e.tensor_scalar(mask[:, :], rank[:, :, :].rearrange("p j n -> p (j n)"), 1.5, None,
                                ALU.is_lt).then_inc(s["v_mask"], 1)

            def mask_out(b):
                after(e, "t_mask", b)
                if b.known(1, BLOCKS):
                    e.wait_ge(s["st_mk"], 16 * b.index)
                e.tensor_copy(maskT[:, :], X2[:, :].bitcast(BF16)[0:TILES * EXPERTS, 0:P]
                              ).then_inc(s["v_mT"], 1)

            def body(b):
                prev, nxt = b.known(1, BLOCKS + 1), b.known(0, BLOCKS - 1)
                old = b.known(2, BLOCKS)
                if nxt:
                    stats(b + 1)
                if prev:
                    gru_a(b + -1)
                if nxt:
                    normalize(b + 1)
                if old:
                    choose(b + -2)
                    choose_b(b + -2)
                nmp_lo(b)
                if prev:
                    gru_d(b + -1)
                if nxt:
                    norm_lo(b + 1)
                if old:
                    mask_out(b + -2)
                if prev:
                    gru_b(b + -1)
                if nxt:
                    embed(b + 1)
                    conv1_lo(b + 1)
                    messages(b + 1)
                if prev:
                    stats2(b + -1)
                if nxt:
                    messages_lo(b + 1)
                if prev:
                    normalize2(b + -1)
                if nxt:
                    weights(b + 1)
                conv2_sum(b)
                if nxt:
                    weights_lo(b + 1)
                conv2_lo(b)

            stats(Block(0, 0))
            e.wait_ge(s["k_w1"], 2)
            tt(w1c_lo[:, :], raw_w1c, f32(w1c_hi[:, :]), ALU.subtract, "k_sp_dve")
            tt(wse_lo[:, :], raw_wse, f32(wse_hi[:, :]), ALU.subtract, "k_sp_dve")
            normalize(Block(0, 0))
            e.wait_ge(s["k_bnp"], 1)
            tt(s1[:, :], vec[:, BN1_G:BN1_G + 1], bnr[:, 0:1], ALU.mult, "k_bnr")
            tt(s2[:, :], vec[:, BN2_G:BN2_G + 1], bnr[:, 1:2], ALU.mult, "k_bnr")
            e.wait_ge(s["k_bnr"], 2)
            tt(bnt[:, 0:1], vec[:, BN1_M:BN1_M + 1], s1[:, :], ALU.mult, "k_bnr")
            tt(bnt[:, 1:2], vec[:, BN2_M:BN2_M + 1], s2[:, :], ALU.mult, "k_bnr")
            e.wait_ge(s["k_bnr"], 4)
            tt(o1[:, :], vec[:, BN1_B:BN1_B + 1], bnt[:, 0:1], ALU.subtract, "k_bno")
            tt(o2[:, :], vec[:, BN2_B:BN2_B + 1], bnt[:, 1:2], ALU.subtract, "k_bno")
            norm_lo(Block(0, 0))
            embed(Block(0, 0))
            conv1_lo(Block(0, 0))
            messages(Block(0, 0))
            e.wait_ge(s["k_g"], 1)
            tt(w2c_lo[:, :, :].rearrange("p k n -> p (k n)"), raw_w2c,
               f32(w2c_hi[:, :, :].rearrange("p k n -> p (k n)")), ALU.subtract, "k_sp_dve")
            messages_lo(Block(0, 0))
            weights(Block(0, 0))
            weights_lo(Block(0, 0))
            e.wait_ge(s["k_g"], 2)
            tt(wg_lo[:, :, :].rearrange("p k n -> p (k n)"), raw_wg,
               f32(wg_hi[:, :, :].rearrange("p k n -> p (k n)")), ALU.subtract, "k_sp_dve")
            e.wait_ge(s["ld_c2"], 16 * 3)
            for n in range(3):
                body(Block(0, n))
            pairs_loop(e, 3, (BLOCKS - 4) // 2, body)
            last = Block(0, BLOCKS - 1)
            body(last)

            def split(b):
                f_split_waits(e, b)
                e.wait_ge(s["f_qh"], b.index + 1)
                tt(ql[b.par], y2x[b.par], f32(qh[b.par]), ALU.subtract, "f_ql")

            def hidden_lo(b, x):
                p, n = x % 2, EXPERTS * b.index + x
                for c in range(CH):
                    part = slice(c * BLOCK, (c + 1) * BLOCK)
                    e.wait_ge(s["f_hh"], CH * n + c + 1)
                    if c == 0 and (x >= 2 or b.known(1, BLOCKS)):
                        e.wait_ge(s["f_down"], n - 1)
                    tt(hl[p][:, part], hf[p][:, part], f32(hh[p][:, part]), ALU.subtract, "f_hl")

            def add(b, x):
                p, n = x % 2, EXPERTS * b.index + x
                e.wait_ge(s["f_down"], n + 1)
                if x == 0:
                    loaded(e, "f_mk", b)
                e.scalar_tensor_tensor(out=ym[p], in0=down[p][:, :],
                                       scalar=vec[:, B2_AT + x:B2_AT + x + 1],
                                       in1=maskb[b.par][:, x, :], op0=ALU.add, op1=ALU.mult
                                       ).then_inc(s["f_ym"], 1)
                e.wait_ge(s["f_ym"], n + 1)
                if x == 0:
                    loaded(e, "f_x1", b)
                else:
                    e.wait_ge(s["f_acc"], n)
                tt(x1r[b.par], x1r[b.par], ym[p], ALU.add, "f_acc")

            def turn(b):
                for x in range(EXPERTS):
                    start = isinstance(b.k, int) and b.index == 0
                    if start and x == 1:
                        mask_out(last + -1)
                    if start and x == 3:
                        choose(last)
                        choose_b(last)
                    if start and x == 5:
                        mask_out(last)
                    if x == EXPERTS - 2 and b.known(0, BLOCKS - 1):
                        split(b + 1)
                    if x + 1 < EXPERTS:
                        hidden_lo(b, x + 1)
                    elif b.known(0, BLOCKS - 1):
                        hidden_lo(b + 1, 0)
                    add(b, x)

            after(e, "t_av", last)
            split(Block(0, 0))
            gru_a(last)
            gru_d(last)
            gru_b(last)
            hidden_lo(Block(0, 0), 0)
            choose(last + -1)
            choose_b(last + -1)
            stats2(last)
            normalize2(last)
            turn(Block(0, 0))
            pairs_loop(e, 1, (BLOCKS - 2) // 2, turn)
            turn(Block(0, BLOCKS - 1))

        @blk.tensor
        def _(e):
            def mm3(o, w_hi, w_lo, m_hi, m_lo, first, end):
                e.matmul(o, w_hi, m_hi, start=first, stop=False)
                e.matmul(o, w_hi, m_lo, start=False, stop=False)
                return e.matmul(o, w_lo, m_hi, start=False, stop=end)

            def conv2(b, lo, hi):
                ps = C2[:, :].rearrange("p (g n) -> p g n", g=GP)
                if lo == 0:
                    after(e, "v_h1l", b)
                    after(e, "a_h1h", b)
                    after(e, "v_ct", b + -1)
                for k in range(lo, hi):
                    m = mm3(ps, w2c_hi[:, k, :], w2c_lo[:, k, :], h1h[:, b.par, :, k:k + NODES],
                            h1l[:, b.par, :, k:k + NODES], k == 0, k == TAPS - 1)
                if hi == TAPS:
                    m.then_inc(s["t_conv2"], 1)

            def message_pass(b):
                after(e, "v_ml", b)
                after(e, "v_al", b)
                after(e, "a_u", b + -1)
                for g in range(GP):
                    for m in range(MB):
                        j = g * MB + m
                        q = mm3(PH[:, g * NODES:(g + 1) * NODES], mh[:, j * P:(j + 1) * P],
                                ml[:, j * P:(j + 1) * P], ah[:, j, :], al[:, j, :], m == 0, m == MB - 1)
                q.then_inc(s["t_av"], 1)

            def turn_in(b):
                after(e, "v_norm", b)
                for j in range(TILES):
                    q = e.transpose(X0[:, j * P:(j + 1) * P], xn[:, j, :], ident[:, :])
                q.then_inc(s["t_in"], 1)

            def conv1(b):
                after(e, "a_xnh", b)
                after(e, "v_xnl", b)
                mm3(X1[:, :], w1c_hi[:, :], w1c_lo[:, :], xnh[:, b.par], xnl[:, b.par], True, True
                    ).then_inc(s["t_conv1"], 1)

            def embed(b):
                after(e, "a_xnh", b)
                after(e, "v_xnl", b)
                after(e, "v_mT", b + -3)
                mm3(X2[0:SE, :], wse_hi[:, :], wse_lo[:, :], xnh[:, b.par], xnl[:, b.par], True, True
                    ).then_inc(s["t_s"], 1)

            def messages(b):
                after(e, "a_xnf", b)
                after(e, "a_rt", b + -2)
                for j in range(TILES):
                    q = e.matmul(PR[:, j * P:(j + 1) * P], xnf[:, b.par, j * P:(j + 1) * P],
                                 wmsg[:, :], start=True, stop=True)
                q.then_inc(s["t_msg"], 1)

            def distances(b):
                after(e, "a_sq1", b)
                after(e, "v_l0", b)
                after(e, "a_zt", b + -2)
                after(e, "v_w", b + -2)
                for g, ps in enumerate((PZ, PI)):
                    for m in range(MB):
                        j = g * MB + m
                        q = e.matmul(ps[:, m * NODES:(m + 1) * NODES], L[:, j * P:(j + 1) * P],
                                     R[:, g * NODES:(g + 1) * NODES], start=True, stop=True)
                    q.then_inc(s[f"t_dist{g}"], 1)

            def turn_x1(b):
                after(e, "v_x1", b)
                after(e, "v_xnl", b + 2)
                after(e, "a_xnf", b + 2)
                for j in range(TILES):
                    q = e.transpose(X0[:, j * P:(j + 1) * P], x1[:, j * P:(j + 1) * P], ident[:, :])
                q.then_inc(s["t_x1"], 1)

            def turn_x2(b):
                after(e, "v_norm2", b)
                after(e, "a_h1", b + 2)
                for j in range(TILES):
                    q = e.transpose(X1[:, j * P:(j + 1) * P], xn2[:, j, :], ident[:, :])
                q.then_inc(s["t_x2"], 1)

            def gate(b):
                after(e, "a_x2", b)
                after(e, "v_l0", b + 1)
                after(e, "a_sq1", b + 1)
                for j in range(TILES):
                    q = e.matmul(X2[:, j * P:(j + 1) * P], x2c[:, j * P:(j + 1) * P], wgate[:, :],
                                 start=True, stop=True)
                q.then_inc(s["t_gate"], 1)

            def gru(b):
                end = isinstance(b.k, int) and b.index == BLOCKS - 1
                xh, xl = xnh[:, b.par], xnl[:, b.par]

                def part(ps, w, g, m_hi, m_lo, first, last):
                    return mm3(ps[:, :], wg_hi[:, w, g * D:(g + 1) * D], wg_lo[:, w, g * D:(g + 1) * D],
                               m_hi, m_lo, first, last)

                if isinstance(b.k, int) and b.index == 0:
                    e.wait_ge(s["k_sp_dve"], 4)
                    e.wait_ge(s["k_g"], 2)
                if end:
                    after(e, "a_rt", b + -1)
                    after(e, "a_zt", b + -1)
                    after(e, "v_w", b + -1)
                after(e, "v_mt", b + 1)
                after(e, "a_e1", b + 1)
                after(e, "a_nh", b)
                after(e, "v_nl", b)
                part(PH, 2, 2, xh, xl, True, True).then_inc(s["t_gh"], 1)
                part(PR, 2, 0, xh, xl, True, False)
                part(PZ, 2, 1, xh, xl, True, False)
                if b.known(1, BLOCKS):
                    turn_x2(b + -1)
                part(PR, 1, 0, nh[:, :], nl[:, :], False, False)
                part(PZ, 1, 1, nh[:, :], nl[:, :], False, False)
                part(PI, 1, 2, nh[:, :], nl[:, :], True, False)
                after(e, "a_ch", b)
                after(e, "v_cl", b)
                part(PR, 0, 0, chh[:, :], cl[:, :], False, True).then_inc(s["t_r"], 1)
                part(PZ, 0, 1, chh[:, :], cl[:, :], False, True).then_inc(s["t_z"], 1)
                part(PI, 0, 2, chh[:, :], cl[:, :], False, True).then_inc(s["t_n"], 1)

            def turn_mask(b):
                after(e, "v_mask", b)
                after(e, "v_gs", b)
                e.transpose(X2[:, :].bitcast(BF16)[0:TILES * EXPERTS, 0:P], mask[:, :], identb[:, :]
                            ).then_inc(s["t_mask"], 1)

            def body(b):
                prev, nxt = b.known(1, BLOCKS + 1), b.known(0, BLOCKS - 1)
                old = b.known(2, BLOCKS)
                if old:
                    gate(b + -2)
                conv2(b, 0, 4)
                message_pass(b)
                conv2(b, 4, 6)
                if nxt:
                    turn_in(b + 1)
                if old:
                    turn_mask(b + -2)
                conv2(b, 6, 10)
                if nxt:
                    embed(b + 1)
                    conv1(b + 1)
                    messages(b + 1)
                if prev:
                    turn_x1(b + -1)
                conv2(b, 10, 13)
                if nxt:
                    distances(b + 1)
                conv2(b, 13, TAPS)
                gru(b)

            e.wait_ge(s["ld_c"], 64)
            turn_in(Block(0, 0))
            e.wait_ge(s["k_sp_dve"], 2)
            embed(Block(0, 0))
            conv1(Block(0, 0))
            messages(Block(0, 0))
            e.wait_ge(s["k_ones"], 2)
            distances(Block(0, 0))
            e.wait_ge(s["k_sp_dve"], 3)
            e.wait_ge(s["k_g"], 1)
            body(Block(0, 0))
            e.wait_ge(s["ld_c2"], 16 * 3)
            e.wait_ge(s["k_id"], 1)
            body(Block(0, 1))
            body(Block(0, 2))
            pairs_loop(e, 3, (BLOCKS - 4) // 2, body)
            last = Block(0, BLOCKS - 1)
            body(last)

            def up_proj(b, x):
                p, n = x % 2, EXPERTS * b.index + x
                if x == 0:
                    e.wait_ge(s["f_qh"], b.index + 1)
                    e.wait_ge(s["f_ql"], b.index + 1)
                if x >= 2 or b.known(1, BLOCKS):
                    e.wait_ge(s["f_h"], CH * (n - 1))
                for c in range(CH):
                    mm3(up[p][c][:, :], wu_hi[:, x, c * P:(c + 1) * P], wu_lo[:, x, c * P:(c + 1) * P],
                        qh[b.par], ql[b.par], True, True).then_inc(s["f_up"], 1)

            def down_proj(b, x):
                p, n = x % 2, EXPERTS * b.index + x
                if x >= 2 or b.known(1, BLOCKS):
                    e.wait_ge(s["f_ym"], n - 1)
                for c in range(CH):
                    e.wait_ge(s["f_hl"], CH * n + c + 1)
                    q = mm3(down[p][:, :], wd_hi[:, x, c, :], wd_lo[:, x, c, :],
                            hh[p][:, c * BLOCK:(c + 1) * BLOCK], hl[p][:, c * BLOCK:(c + 1) * BLOCK],
                            c == 0, c == CH - 1)
                q.then_inc(s["f_down"], 1)

            def turn(b):
                start = isinstance(b.k, int) and b.index == 0
                for x in range(EXPERTS):
                    if x + 1 < EXPERTS:
                        up_proj(b, x + 1)
                    elif b.known(0, BLOCKS - 1):
                        up_proj(b + 1, 0)
                    if start and x == 0:
                        gate(last + -1)
                    if start and x == 0:
                        turn_x1(last)
                    if start and x == 1:
                        turn_mask(last + -1)
                    if start and x == 2:
                        turn_x2(last)
                    if start and x == 3:
                        after(e, "v_mT", last + -1)
                        gate(last)
                    if start and x == 5:
                        turn_mask(last)
                    down_proj(b, x)

            e.wait_ge(s["k_ff"], 4)
            after(e, "a_rt", last)
            after(e, "a_zt", last)
            up_proj(Block(0, 0), 0)
            after(e, "v_w", last)
            after(e, "a_u", last)
            turn(Block(0, 0))
            pairs_loop(e, 1, (BLOCKS - 2) // 2, turn)
            turn(Block(0, BLOCKS - 1))


def kernel(**inputs):
    import numpy as np
    import concourse.bacc as bacc
    from concourse.bass_utils import run_bass_kernel_spmd as run

    v = {k: np.asarray(x) for k, x in inputs.items()}
    gnn = lambda n: v["L0_gnn_" + n]
    ffn = lambda n: v["L0_ffn_" + n]
    tokens = GRAPHS * NODES
    wse = np.zeros((D, SE), np.float32)
    bse = np.zeros((P,), np.float32)
    for at in range(0, SE, 32):
        wse[:, at:at + 3] = gnn("w_se").T
        bse[at:at + 3] = gnn("b_se")
    w_ih, w_hh = gnn("w_ih"), gnn("w_hh")
    wgate = np.zeros((D, P), np.float32)
    wgate[:, :EXPERTS] = ffn("Wg")
    cols = [gnn(f"bn{n}_{c}") for n in (1, 2) for c in "gbmv"]
    cols += [gnn(w)[n * D:(n + 1) * D] for w in ("b_ih", "b_hh") for n in range(3)] + [bse]
    cols += list(ffn("b1").reshape(EXPERTS * CH, P)) + list(ffn("b2"))
    arrays = {
        "x": v["x"].reshape(tokens, D),
        "xT": v["x"].reshape(tokens, D).T,
        "adjT": v["adj"].transpose(0, 2, 1).reshape(tokens, NODES),
        "conv1": gnn("conv1_w")[:, :, 0].T,
        "conv2": gnn("conv2_w").transpose(1, 2, 0).reshape(D, TAPS * D),
        "wse": wse,
        "wgru": np.concatenate([w_ih[:, :D].T, w_ih[:, D:].T, w_hh.T], axis=1),
        "wmsg": gnn("w_msg").T,
        "wgate": wgate,
        "wup": ffn("W1").transpose(1, 0, 2).reshape(D, EXPERTS * HID),
        "wdown": ffn("W2").reshape(EXPERTS, CH, P, D).transpose(2, 0, 1, 3).reshape(P, -1),
        "vec": np.stack(cols, axis=1),
        "bmsg": np.broadcast_to(np.tile(gnn("b_msg"), TILES), (P, TILES * D)),
        "bgate": np.broadcast_to(np.tile(ffn("bg"), TILES), (P, TILES * EXPERTS)),
        "ident": np.eye(P, dtype=np.float32),
        "earlier": np.broadcast_to(np.tril(np.ones((EXPERTS, EXPERTS), np.float32), -1),
                                   (P, EXPERTS, EXPERTS)),
    }
    arrays = {k: np.ascontiguousarray(x) for k, x in arrays.items()}
    nc = bacc.Bacc("TRN2", target_bir_lowering=False, num_devices=1)
    aps = {k: nc.dram_tensor(f"in_{k}", x.shape, mybir.dt.from_np(x.dtype), kind="ExternalInput").ap()
           for k, x in arrays.items()}
    out = nc.dram_tensor("outT", [P, tokens], F32, kind="ExternalOutput").ap()
    build(nc, aps, out)
    r = run(nc, [{f"in_{k}": x for k, x in arrays.items()}], core_ids=[0])
    return np.ascontiguousarray(r.results[0]["outT"].T).reshape(GRAPHS, NODES, D)
```

```python
from contextlib import ExitStack

import concourse.bass as bass
from concourse import mybir

F32 = mybir.dt.float32
F32R = mybir.dt.float32r
BF16 = mybir.dt.bfloat16
ALU = mybir.AluOpType
ACT = mybir.ActivationFunctionType
AX = mybir.AxisListType

P = 128
GRAPHS, NODES, D = 32, 256, 128
GP = 2
BLOCK = GP * NODES
TILES = BLOCK // P
MB = NODES // P
BLOCKS = GRAPHS // GP
TAPS, PAD = 17, 8
WIDE = NODES + 2 * PAD
EXPERTS, HID = 8, 256
CH = HID // P
EPS = 1e-5
COORDS = 3
MSG = D + COORDS
C1S, C2S, C4S = COORDS, 2 * COORDS, 4 * COORDS
FACTORS = C4S + 4
RIGHT = 32

(BN1_G, BN1_B, BN1_M, BN1_V, BN2_G, BN2_B, BN2_M, BN2_V, BIH_R, BIH_Z, BIH_N, BHH_R, BHH_Z,
 BHH_N) = range(14)
B1_AT = 14
B2_AT = B1_AT + EXPERTS * CH
NVEC = B2_AT + EXPERTS


class Block:

    def __init__(self, k, off):
        self.k, self.off = k, off

    def __add__(self, n):
        return Block(self.k, self.off + n)

    @property
    def index(self):
        return 2 * self.k + self.off

    @property
    def par(self):
        return self.off % 2

    @property
    def half(self):
        return self.k + self.off // 2

    def known(self, low, high):
        return not isinstance(self.k, int) or low <= self.index < high


def build(nc, a, out):
    ctx = ExitStack()
    with ctx:
        def sb(name, shape, dt=F32):
            return ctx.enter_context(nc.sbuf_tensor(name, shape, dt))

        def sem(name):
            return ctx.enter_context(nc.semaphore(name))

        w2c_hi = sb("w2c_hi", [P, TAPS, D], F32R)
        w2c_lo = sb("w2c_lo", [P, TAPS, D], F32R)
        w1c_hi = sb("w1c_hi", [P, D], F32R)
        w1c_lo = sb("w1c_lo", [P, D], F32R)
        wg_hi = sb("wgru_hi", [P, 3, 3 * D], F32R)
        wg_lo = sb("wgru_lo", [P, 3, 3 * D], F32R)
        wmsg = sb("wmsg", [P, MSG])
        wgate = sb("wgate", [P, P])
        wu_hi = sb("wup_hi", [P, EXPERTS, HID], F32R)
        wu_lo = sb("wup_lo", [P, EXPERTS, HID], F32R)
        wd_hi = sb("wdown_hi", [P, EXPERTS, CH, D], F32R)
        wd_lo = sb("wdown_lo", [P, EXPERTS, CH, D], F32R)
        vec = sb("vec", [P, NVEC])
        bmsg = sb("bmsg", [P, TILES // 2, MSG])
        bgate = sb("bgate", [P, TILES * EXPERTS])
        ident = sb("ident", [P, P])
        identb = sb("identb", [P, P], BF16)
        earlier = sb("earlier", [P, EXPERTS, EXPERTS])
        halfpow = sb("halfpow", [P, 8])
        bnv = sb("bnv", [P, 2])
        bnr = sb("bnr", [P, 2])
        bnt = sb("bnt", [P, 2])
        spare = sb("spare", [P, 1])
        s1 = sb("s1", [P, 1])
        o1 = sb("o1", [P, 1])
        s2 = sb("s2", [P, 1])
        o2 = sb("o2", [P, 1])
        hb = sb("hb", [P, 3])
        STAGE = TAPS * D + 2 * EXPERTS * HID + 9 * D + D
        stage = sb("stage", [P, STAGE])
        at = [0]

        def view(n, dt=F32):
            lo = at[0]
            at[0] += n
            v = stage[:, lo:lo + n]
            return v if dt is F32 else v.bitcast(dt)

        raw_w2c = view(TAPS * D)
        raw_w1c = view(D)
        raw_wg = view(9 * D)
        raw_wu = view(EXPERTS * HID)
        raw_wd = view(EXPERTS * HID)
        at[0] = 0
        maskb = [view(EXPERTS * BLOCK // 2, BF16).rearrange("p (e t) -> p e t", e=EXPERTS)
                 for _ in range(2)]
        y2x = [view(BLOCK) for _ in range(2)]
        x1r = [view(BLOCK) for _ in range(2)]
        ym = [view(BLOCK) for _ in range(2)]
        assert at[0] <= STAGE

        xt = sb("xtok", [P, 2, TILES, D])
        adj = sb("adj", [P, 2, TILES, NODES])
        xT = sb("xT", [P, 2, BLOCK])
        st = sb("st", [P, TILES, 6])
        mv = sb("mv", [P, TILES, 2])
        ve = sb("ve", [P, TILES])
        rs = sb("rs", [P, TILES])
        st2 = sb("st2", [P, TILES, 6])
        mv2 = sb("mv2", [P, TILES, 2])
        ve2 = sb("ve2", [P, TILES])
        rs2 = sb("rs2", [P, TILES])
        xn = sb("xn", [P, TILES, D])
        xnf = sb("xnT", [P, 2, BLOCK])
        xnh = sb("xnT_hi", [P, 2, BLOCK], F32R)
        xnl = sb("xnT_lo", [P, 2, BLOCK], F32R)
        h1f = sb("h1", [P, GP, NODES])
        h1h = sb("h1_hi", [P, 2, GP, WIDE], F32R)
        h1l = sb("h1_lo", [P, 2, GP, WIDE], F32R)
        sq3 = sb("sq3", [P, TILES, COORDS])
        sq = sb("sq", [P, TILES, 1])
        fac = sb("factors", [P, TILES, P], F32R)
        fl = sb("factors_left", [FACTORS, BLOCK], F32R)
        fr = sb("factors_right", [FACTORS, BLOCK], F32R)
        am = sb("am", [P, TILES, NODES])
        ah = sb("a_hi", [P, TILES, NODES], F32R)
        al = sb("a_lo", [P, TILES, NODES], F32R)
        mt = sb("mt", [P, TILES, MSG])
        mf = sb("msg", [P, TILES * D])
        mh = sb("msg_hi", [P, BLOCK], F32R)
        ml = sb("msg_lo", [P, BLOCK], F32R)
        nh = sb("nmp_hi", [P, BLOCK], F32R)
        nl = sb("nmp_lo", [P, BLOCK], F32R)
        ct = sb("ct", [P, BLOCK])
        cf = sb("xconv", [P, BLOCK])
        chh = sb("xconv_hi", [P, BLOCK], F32R)
        cl = sb("xconv_lo", [P, BLOCK], F32R)
        rt = sb("rt", [P, BLOCK])
        zt = sb("zt", [P, BLOCK])
        uu = sb("uu", [P, BLOCK])
        vv = sb("vv", [P, BLOCK])
        nn = sb("nn", [P, BLOCK])
        dd = sb("dd", [P, BLOCK])
        x1 = sb("x1T", [P, BLOCK])
        xn2 = sb("xn2", [P, TILES, D])
        x2c = sb("xn2T", [P, BLOCK])
        gs = sb("gs", [P, TILES, EXPERTS])
        cmp_ = sb("cmp", [P, TILES, EXPERTS, EXPERTS])
        ceq = sb("ceq", [P, TILES, EXPERTS, EXPERTS])
        rank = sb("rank", [P, TILES, EXPERTS])
        mask = sb("mask", [P, TILES * EXPERTS], BF16)
        maskT = sb("maskT", [TILES * EXPERTS, P], BF16)

        hf = [am[:, :, :].rearrange("p t n -> p (t n)"),
              xnf[:, :, :].rearrange("p t n -> p (t n)")]
        hh = [ah[:, :, :].rearrange("p t n -> p (t n)"), al[:, :, :].rearrange("p t n -> p (t n)")]
        hl = [xnh[:, :, :].rearrange("p t n -> p (t n)"), xnl[:, :, :].rearrange("p t n -> p (t n)")]
        qh = [mh[:, :], nh[:, :]]
        ql = [ml[:, :], nl[:, :]]

        banks = [ctx.enter_context(nc.psum_tensor(f"bank{n}", [P, BLOCK], F32)) for n in range(8)]
        X0, X1, X2, C2, PR, PZ, PI, PH = banks
        up = [[PR, PZ], [PI, PH]]
        down = [C2, X0]

        d_x1 = nc.dram_tensor("kept_x1", [P, GRAPHS * NODES], F32, kind="Internal").ap()
        d_x2 = nc.dram_tensor("kept_xn2", [P, GRAPHS * NODES], F32, kind="Internal").ap()
        d_mk = nc.dram_tensor("kept_mask", [EXPERTS, GRAPHS * NODES], BF16, kind="Internal").ap()

        def f32(ap):
            return ap.bitcast(F32)

        names = """ld_x0 ld_x1 ld_adj0 ld_adj1 ld_t0 ld_t1 ld_w2c ld_w1 ld_g ld_ff ld_c ld_c2 ld_id st_x1 st_x2
            st_mk k_init k_half k_sp_dve k_w1 k_g k_ff_hi k_ff k_bn k_bnp k_bnr k_bno k_hb k_id k_ones
            v_st v_agg v_var v_norm p_rs v_rs2 p_rs2 v_st2 v_agg2
            t_in t_conv1 t_msg t_fac t_dist0 t_dist1 t_av t_x1 t_x2 t_conv2 t_gate t_gh t_r t_z t_n
            t_mask a_xnh a_xnf a_h1 a_h1h a_fl a_fr a_msg a_msgh a_e0 a_e1 a_ah a_nh a_c a_ch a_rt
            a_zt a_u a_nn a_x2 v_xnl v_h1l v_s_hi v_s_sq v_s_lo v_sq v_sq_hi v_sq_lo v_fac v_mt v_ml v_am v_al v_nl v_ct v_cl v_v v_w v_d
            v_e v_g v_x1 v_norm2 v_gs v_cmp v_ceq v_sum v_rank v_mask v_mT
            f_mk0 f_mk1 f_x20 f_x21 f_x10 f_x11 f_qh f_ql f_up f_h f_hh f_hl f_down f_ym f_acc
            f_out""".split()
        s = {n: sem(n) for n in names}

        def after(e, name, b):
            if b.known(0, BLOCKS):
                e.wait_ge(s[name], b.index + 1)

        def loaded(e, name, b):
            e.wait_ge(s[f"{name}{b.par}"], 16 * (b.half + 1))

        def tok(ap, b):
            return ap[:, bass.ds(b.index * BLOCK, BLOCK)]

        x_d = a["x"].rearrange("(b j p) d -> b p j d", j=TILES, p=P)
        adj_d = a["adjT"].rearrange("(b j p) n -> b p j n", j=TILES, p=P)

        ctx2 = ctx.enter_context(nc.Block())
        blk = ctx2

        def pairs_loop(e, first, rounds, body):
            with e.Fori(0, rounds) as k:
                body(Block(k, first))
                body(Block(k, first + 1))

        @blk.sync
        def _(e):
            def load_x(b):
                after(e, "v_norm", b + -2)
                e.dma_start(xt[:, b.par], x_d[b.index]).then_inc(s[f"ld_x{b.par}"], 16)

            def load_adj(b):
                after(e, "v_am", b + -2)
                e.dma_start(adj[:, b.par], adj_d[b.index]).then_inc(s[f"ld_adj{b.par}"], 16)

            def load_xT(b):
                after(e, "v_x1", b + -2)
                e.dma_start(xT[:, b.par], tok(a["xT"], b)).then_inc(s[f"ld_t{b.par}"], 16)

            def keep_x1(b):
                after(e, "v_x1", b)
                e.dma_start(tok(d_x1, b), x1[:, :]).then_inc(s["st_x1"], 16)

            def store_mask(b):
                e.dma_start(tok(d_mk, b).rearrange("e (j t) -> j e t", j=TILES),
                            maskT[:, :]).then_inc(s["st_mk"], 16)

            def keep_x2(b):
                after(e, "v_mT", b + -1)
                after(e, "a_x2", b)
                e.dma_start(tok(d_x2, b), x2c[:, :]).then_inc(s["st_x2"], 16)
                if b.known(1, BLOCKS):
                    store_mask(b + -1)

            def body(b):
                if b.known(0, BLOCKS - 2):
                    load_x(b + 2)
                    load_adj(b + 2)
                if b.known(1, BLOCKS):
                    keep_x1(b + -1)
                if b.known(0, BLOCKS - 1):
                    load_xT(b + 1)
                if b.known(1, BLOCKS):
                    keep_x2(b + -1)

            load_x(Block(0, 0))
            e.dma_start(ident[:, :], a["ident"]).then_inc(s["ld_id"], 16)
            e.dma_start(raw_w1c, a["conv1"]).then_inc(s["ld_w1"], 16)
            e.dma_start(vec[:, :], a["vec"]).then_inc(s["ld_c"], 16)
            e.dma_start(wmsg[:, :], a["wmsg"]).then_inc(s["ld_c"], 16)
            e.dma_start(bmsg[:, :, :], a["bmsg"]).then_inc(s["ld_c"], 16)
            load_adj(Block(0, 0))
            e.dma_start(raw_w2c, a["conv2"]).then_inc(s["ld_w2c"], 16)
            load_x(Block(0, 1))
            e.dma_start(raw_wg, a["wgru"]).then_inc(s["ld_g"], 16)
            load_xT(Block(0, 0))
            load_adj(Block(0, 1))
            e.dma_start(wgate[:, :], a["wgate"]).then_inc(s["ld_c2"], 16)
            e.dma_start(bgate[:, :], a["bgate"]).then_inc(s["ld_c2"], 16)
            e.dma_start(earlier[:, :, :], a["earlier"]).then_inc(s["ld_c2"], 16)
            e.dma_start(raw_wu, a["wup"]).then_inc(s["ld_ff"], 16)
            e.dma_start(raw_wd, a["wdown"]).then_inc(s["ld_ff"], 16)
            def fetch(b):
                e.wait_ge(s["st_x1"], 16 * (b.index + 1))
                e.wait_ge(s["st_x2"], 16 * (b.index + 1))
                e.wait_ge(s["st_mk"], 16 * (b.index + 1))
                if b.known(2, BLOCKS):
                    e.wait_ge(s["f_ql"], b.index - 1)
                    e.wait_ge(s["f_qh"], b.index - 1)
                e.dma_start(y2x[b.par], tok(d_x2, b)).then_inc(s[f"f_x2{b.par}"], 16)
                e.dma_start(maskb[b.par], tok(d_mk, b).unsqueeze(0).broadcast_to([P, EXPERTS, BLOCK])
                            ).then_inc(s[f"f_mk{b.par}"], 16)
                if b.known(2, BLOCKS):
                    e.wait_ge(s["f_out"], 16 * (b.index - 1))
                e.dma_start(x1r[b.par], tok(d_x1, b)).then_inc(s[f"f_x1{b.par}"], 16)

            def store(b):
                e.wait_ge(s["f_acc"], EXPERTS * (b.index + 1))
                e.dma_start(tok(out, b), x1r[b.par]).then_inc(s["f_out"], 16)

            def turn(b):
                store(b)
                if b.known(0, BLOCKS - 2):
                    fetch(b + 2)

            body(Block(0, 0))
            body(Block(0, 1))
            pairs_loop(e, 2, (BLOCKS - 4) // 2, body)
            e.wait_ge(s["k_ff"], 4)
            e.wait_ge(s["k_sp_dve"], 3)
            fetch(Block(0, 0))
            fetch(Block(0, 1))
            body(Block(0, BLOCKS - 2))
            body(Block(0, BLOCKS - 1))
            last = Block(0, BLOCKS - 1)
            keep_x1(last)
            turn(Block(0, 0))
            keep_x2(last)
            turn(Block(0, 1))
            after(e, "v_mT", last)
            store_mask(last)
            pairs_loop(e, 2, (BLOCKS - 4) // 2, turn)
            turn(Block(0, BLOCKS - 2))
            turn(Block(0, BLOCKS - 1))
            e.wait_ge(s["f_out"], 16 * BLOCKS)

        @blk.gpsimd
        def _(e):
            e.memset(halfpow[:, :], -0.5).then_inc(s["k_half"], 1)
            e.wait_ge(s["k_half"], 1)

            def root(b):
                after(e, "v_var", b)
                after(e, "v_norm", b + -1)
                e.tensor_tensor(rs[:, :], ve[:, :], halfpow[:, 0:TILES], ALU.pow).then_inc(s["p_rs"], 1)

            def root2(b):
                after(e, "v_rs2", b)
                after(e, "v_norm2", b + -1)
                e.tensor_tensor(rs2[:, :], ve2[:, :], halfpow[:, 0:TILES], ALU.pow).then_inc(s["p_rs2"], 1)

            def body(b):
                first = isinstance(b.k, int) and b.index < PIECES
                if b.known(0, BLOCKS - 1):
                    root(b + 1)
                if first:
                    split_piece(b.index)
                if b.known(1, BLOCKS + 1):
                    root2(b + -1)

            flat = [t[:, :, :].rearrange("p e n -> p (e n)") for t in (wu_hi, wu_lo)] + \
                   [t[:, :, :, :].rearrange("p e c n -> p (e c n)") for t in (wd_hi, wd_lo)]
            PIECES = 2
            width = EXPERTS * HID // PIECES

            def split_piece(i):
                if i == 0:
                    e.wait_ge(s["ld_ff"], 32)
                for m, raw in enumerate((raw_wu, raw_wd)):
                    part = slice(i * width, (i + 1) * width)
                    e.tensor_copy(flat[2 * m][:, part], raw[:, part]).then_inc(s["k_ff_hi"], 1)
                    e.wait_ge(s["k_ff_hi"], 2 * i + m + 1)
                    e.tensor_tensor(flat[2 * m + 1][:, part], raw[:, part], f32(flat[2 * m][:, part]),
                                    ALU.subtract).then_inc(s["k_ff"], 1)

            root(Block(0, 0))
            e.wait_ge(s["k_bn"], 2)
            e.tensor_tensor(bnr[:, :], bnv[:, :], halfpow[:, 0:2], ALU.pow).then_inc(s["k_bnp"], 1)
            e.memset(h1h[:, :, :, :].bitcast(F32), 0.0).then_inc(s["k_init"], 1)
            e.memset(h1l[:, :, :, :].bitcast(F32), 0.0).then_inc(s["k_init"], 1)
            for n in range(3):
                body(Block(0, n))
            pairs_loop(e, 3, (BLOCKS - 4) // 2, body)
            body(Block(0, BLOCKS - 1))

            def split(b):
                if b.known(2, BLOCKS):
                    e.wait_ge(s["f_up"], CH * EXPERTS * (b.index - 1))
                e.wait_ge(s["f_qh"], b.index + 1)
                e.tensor_tensor(ql[b.par], y2x[b.par], f32(qh[b.par]), ALU.subtract
                                ).then_inc(s["f_ql"], 1)

            last = Block(0, BLOCKS - 1)
            after(e, "t_av", last)
            split(Block(0, 0))
            root2(last)
            after(e, "t_n", last)
            split(Block(0, 1))
            pairs_loop(e, 2, (BLOCKS - 2) // 2, split)

        @blk.scalar
        def _(e):
            def act(o, i, f, sig, **kw):
                return e.activation(o, i, f, **kw).then_inc(s[sig], 1)

            e.wait_ge(s["ld_w1"], 16)
            act(w1c_hi[:, :], raw_w1c, ACT.Copy, "k_w1")

            def gru(b):
                after(e, "t_gh", b)
                after(e, "v_v", b + -1)
                act(uu[:, :], PH[:, :], ACT.Identity, "a_u", scale=0.5, bias=hb[:, 2:3])
                after(e, "t_r", b)
                act(rt[:, :], PR[:, :], ACT.Tanh, "a_rt", scale=0.5, bias=hb[:, 0:1])
                after(e, "t_z", b)
                after(e, "v_e", b + -1)
                act(zt[:, :], PZ[:, :], ACT.Tanh, "a_zt", scale=0.5, bias=hb[:, 1:2])
                after(e, "v_w", b)
                after(e, "v_g", b + -1)
                act(nn[:, :], vv[:, :], ACT.Tanh, "a_nn", bias=vec[:, BIH_N:BIH_N + 1])

            def nmp_hi(b):
                after(e, "t_av", b)
                after(e, "t_n", b + -1)
                act(nh[:, :], PH[:, :], ACT.Copy, "a_nh")

            def norm_out(b):
                after(e, "t_in", b)
                after(e, "t_n", b + -2)
                after(e, "v_d", b + -2)
                act(xnh[:, b.par], X0[:, :], ACT.Copy, "a_xnh")
                act(xnf[:, b.par], X0[:, :], ACT.Copy, "a_xnf")

            def conv1_out(b):
                after(e, "t_conv1", b)
                if isinstance(b.k, int) and b.index == 0:
                    e.wait_ge(s["k_bno"], 2)
                    e.wait_ge(s["k_init"], 2)
                kw = dict(scale=s1[:, 0:1], bias=o1[:, 0:1])
                ps = X1[:, :].rearrange("p (g n) -> p g n", g=GP)
                after(e, "t_conv2", b + -2)
                act(h1h[:, b.par, :, PAD:PAD + NODES], ps, ACT.Relu, "a_h1h", **kw)
                after(e, "v_h1l", b + -1)
                act(h1f[:, :, :], ps, ACT.Relu, "a_h1", **kw)

            def factors(b):
                after(e, "t_fac", b)
                after(e, "t_dist1", b + -1)
                act(fl[:, :], X1[0:FACTORS, :], ACT.Copy, "a_fl")
                act(fr[:, :], X1[RIGHT:RIGHT + FACTORS, :], ACT.Copy, "a_fr")

            def messages(b):
                after(e, "v_mt", b)
                after(e, "t_av", b + -1)
                m = mt[:, :, 0:D]
                act(mh[:, :].rearrange("p (j d) -> p j d", j=TILES), m, ACT.Relu, "a_msgh")
                after(e, "v_ml", b + -1)
                act(mf[:, :].rearrange("p (j d) -> p j d", j=TILES), m, ACT.Relu, "a_msg")

            def weights_of(b):
                after(e, "v_al", b + -1)
                after(e, "a_ah", b + -1)
                for g, ps in enumerate((PZ, PI)):
                    after(e, f"t_dist{g}", b)
                    act(am[:, g * MB:(g + 1) * MB, :], ps[:, :].rearrange("p (m n) -> p m n", m=MB),
                        ACT.Exp, f"a_e{g}", scale=-1.0)

            def weights_hi(b):
                after(e, "v_am", b)
                after(e, "t_av", b + -1)
                act(ah[:, :, :], am[:, :, :], ACT.Copy, "a_ah")

            def norm2_out(b):
                after(e, "t_x2", b)
                after(e, "t_gate", b + -1)
                if b.known(1, BLOCKS):
                    e.wait_ge(s["st_x2"], 16 * b.index)
                act(x2c[:, :], X1[:, :], ACT.Copy, "a_x2")

            def conv2_out(b):
                after(e, "v_ct", b)
                after(e, "t_n", b + -1)
                act(chh[:, :], ct[:, :], ACT.Relu, "a_ch", bias=o2[:, 0:1])
                after(e, "v_cl", b + -1)
                act(cf[:, :], ct[:, :], ACT.Relu, "a_c", bias=o2[:, 0:1])

            def body(b):
                prev, nxt = b.known(1, BLOCKS + 1), b.known(0, BLOCKS - 1)
                if prev:
                    gru(b + -1)
                nmp_hi(b)
                if nxt:
                    norm_out(b + 1)
                    conv1_out(b + 1)
                    messages(b + 1)
                    factors(b + 1)
                    weights_of(b + 1)
                conv2_out(b)
                if nxt:
                    weights_hi(b + 1)
                if prev:
                    norm2_out(b + -1)

            norm_out(Block(0, 0))
            e.wait_ge(s["ld_w2c"], 16)
            act(w2c_hi[:, :, :].rearrange("p k n -> p (k n)"), raw_w2c, ACT.Copy, "k_g")
            conv1_out(Block(0, 0))
            messages(Block(0, 0))
            factors(Block(0, 0))
            weights_of(Block(0, 0))
            weights_hi(Block(0, 0))
            e.wait_ge(s["ld_g"], 16)
            act(wg_hi[:, :, :].rearrange("p k n -> p (k n)"), raw_wg, ACT.Copy, "k_g")
            for n in range(3):
                body(Block(0, n))
            pairs_loop(e, 3, (BLOCKS - 4) // 2, body)
            body(Block(0, BLOCKS - 1))

            def hidden(b, x):
                p, n = x % 2, EXPERTS * b.index + x
                old = x >= 2 or b.known(1, BLOCKS)
                for c in range(CH):
                    part = slice(c * BLOCK, (c + 1) * BLOCK)
                    e.wait_ge(s["f_up"], CH * n + c + 1)
                    if old and c == 0:
                        e.wait_ge(s["f_hl"], CH * (n - 1))
                    act(hf[p][:, part], up[p][c][:, :], ACT.Gelu, "f_h",
                        bias=vec[:, B1_AT + x * CH + c:B1_AT + x * CH + c + 1])
                    e.wait_ge(s["f_h"], CH * n + c + 1)
                    if old and c == 0:
                        e.wait_ge(s["f_down"], n - 1)
                    act(hh[p][:, part], hf[p][:, part], ACT.Copy, "f_hh")

            def split_hi(b):
                loaded(e, "f_x2", b)
                if b.known(2, BLOCKS):
                    e.wait_ge(s["f_up"], CH * EXPERTS * (b.index - 1))
                act(qh[b.par], y2x[b.par], ACT.Copy, "f_qh")

            def turn(b):
                for x in range(EXPERTS):
                    if isinstance(b.k, int) and b.index == 0 and x == 6:
                        norm2_out(Block(0, BLOCKS - 1))
                    if x == 4 and b.known(0, BLOCKS - 1):
                        split_hi(b + 1)
                    hidden(b, x)

            last = Block(0, BLOCKS - 1)
            after(e, "t_av", last)
            split_hi(Block(0, 0))
            gru(last)
            after(e, "t_n", last)
            after(e, "v_d", last)
            for n in range(3):
                turn(Block(0, n))
            pairs_loop(e, 3, (BLOCKS - 4) // 2, turn)
            turn(Block(0, BLOCKS - 1))

        @blk.vector
        def _(e):
            def tt(o, i, j, op, sig):
                return e.tensor_tensor(o, i, j, op).then_inc(s[sig], 1)

            e.memset(f32(fac[:, :, :]), 1.0).then_inc(s["k_ones"], 1)

            def settled(e, name, b):
                after(e, name, b)
                e.memset(spare[:, :], 0.0)

            def stats(b):
                loaded(e, "ld_x", b)
                after(e, "v_agg", b + -1)
                for j in range(TILES):
                    q = e.bn_stats(st[:, j, :], xt[:, b.par, j, :])
                q.then_inc(s["v_st"], 1)
                settled(e, "v_st", b)
                for j in range(TILES):
                    q = e.bn_aggr(mv[:, j, :], st[:, j, :])
                q.then_inc(s["v_agg"], 1)
                after(e, "v_agg", b)
                after(e, "p_rs", b + -1)
                e.tensor_scalar(ve[:, :], mv[:, :, 1], EPS, None, ALU.add).then_inc(s["v_var"], 1)

            def normalize(b):
                after(e, "p_rs", b)
                after(e, "t_in", b + -1)
                for j in range(TILES):
                    q = e.tensor_scalar(xn[:, j, :], xt[:, b.par, j, :], mv[:, j, 0:1],
                                        rs[:, j:j + 1], ALU.subtract, ALU.mult)
                q.then_inc(s["v_norm"], 1)

            def gru_a(b):
                after(e, "a_u", b)
                after(e, "a_rt", b)
                after(e, "a_nn", b + -1)
                e.scalar_tensor_tensor(out=vv[:, :], in0=rt[:, :], scalar=1.0, in1=uu[:, :],
                                       op0=ALU.add, op1=ALU.mult).then_inc(s["v_v"], 1)
                after(e, "v_v", b)
                after(e, "t_n", b)
                tt(vv[:, :], PI[:, :], vv[:, :], ALU.add, "v_w")

            def gru_d(b):
                after(e, "a_nn", b)
                tt(dd[:, :], xnf[:, b.par], nn[:, :], ALU.subtract, "v_d")

            def gru_b(b):
                after(e, "v_d", b)
                after(e, "a_zt", b)
                e.scalar_tensor_tensor(out=dd[:, :], in0=zt[:, :], scalar=1.0, in1=dd[:, :],
                                       op0=ALU.add, op1=ALU.mult).then_inc(s["v_e"], 1)
                after(e, "v_e", b)
                e.scalar_tensor_tensor(out=dd[:, :], in0=dd[:, :], scalar=0.5, in1=nn[:, :],
                                       op0=ALU.mult, op1=ALU.add).then_inc(s["v_g"], 1)
                after(e, "v_g", b)
                loaded(e, "ld_t", b)
                after(e, "t_x1", b + -1)
                if b.known(1, BLOCKS):
                    e.wait_ge(s["st_x1"], 16 * b.index)
                tt(x1[:, :], dd[:, :], xT[:, b.par], ALU.add, "v_x1")

            def nmp_lo(b):
                after(e, "a_nh", b)
                after(e, "t_n", b + -1)
                tt(nl[:, :], PH[:, :], f32(nh[:, :]), ALU.subtract, "v_nl")

            def norm_lo(b):
                after(e, "a_xnh", b)
                after(e, "a_xnf", b)
                after(e, "t_n", b + -2)
                tt(xnl[:, b.par], X0[:, :], f32(xnh[:, b.par]), ALU.subtract, "v_xnl")

            def conv1_lo(b):
                after(e, "a_h1", b)
                after(e, "a_h1h", b)
                after(e, "t_conv2", b + -2)
                tt(h1l[:, b.par, :, PAD:PAD + NODES], h1f[:, :, :],
                   f32(h1h[:, b.par, :, PAD:PAD + NODES]), ALU.subtract, "v_h1l")

            def messages(b):
                after(e, "t_msg", b)
                after(e, "a_msg", b + -1)
                after(e, "v_fac", b + -1)
                half = TILES // 2
                for n, bank in enumerate((PR, X2)):
                    q = e.tensor_tensor(mt[:, n * half:(n + 1) * half, :],
                                        bank[:, 0:half * MSG].rearrange("p (j d) -> p j d", j=half),
                                        bmsg[:, :, :], ALU.add)
                q.then_inc(s["v_mt"], 1)

            def factors(b):
                def left(lo, hi):
                    return fac[:, :, lo:hi]

                def right(lo, hi):
                    return fac[:, :, RIGHT + lo:RIGHT + hi]

                def twice(ap):
                    return f32(ap).unsqueeze(2).broadcast_to([P, TILES, 2, COORDS])

                emb = mt[:, :, D:MSG]
                after(e, "v_mt", b)
                after(e, "t_fac", b + -1)
                e.tensor_copy(right(0, C1S), emb).then_inc(s["v_s_hi"], 1)
                tt(sq3[:, :, :], emb, emb, ALU.mult, "v_s_sq")
                after(e, "v_s_hi", b)
                tt(right(C1S, C2S), emb, f32(right(0, C1S)), ALU.subtract, "v_s_lo")
                e.tensor_scalar(left(0, C2S).rearrange("p j (r c) -> p j r c", r=2),
                                twice(right(0, C1S)), -2.0, None, ALU.mult)
                after(e, "v_s_sq", b)
                e.tensor_reduce(sq[:, :, :], sq3[:, :, :], AX.X, ALU.add).then_inc(s["v_sq"], 1)
                after(e, "v_s_lo", b)
                e.tensor_scalar(left(C2S, C4S).rearrange("p j (r c) -> p j r c", r=2),
                                twice(right(C1S, C2S)), -2.0, None, ALU.mult)
                after(e, "v_sq", b)
                e.tensor_copy(right(C4S + 2, C4S + 3), sq[:, :, :]).then_inc(s["v_sq_hi"], 1)
                e.tensor_copy(right(C2S, C4S), f32(right(0, C2S)))
                after(e, "v_sq_hi", b)
                tt(right(C4S + 3, C4S + 4), sq[:, :, :], f32(right(C4S + 2, C4S + 3)), ALU.subtract, "v_sq_lo")
                after(e, "v_sq_lo", b)
                e.tensor_copy(left(C4S, C4S + 2), f32(right(C4S + 2, C4S + 4))).then_inc(s["v_fac"], 1)

            def messages_lo(b):
                after(e, "a_msg", b)
                after(e, "t_av", b + -1)
                tt(ml[:, :], mf[:, :], f32(mh[:, :]), ALU.subtract, "v_ml")

            def weights(b):
                after(e, "a_e1", b)
                loaded(e, "ld_adj", b)
                tt(am[:, :, :], am[:, :, :], adj[:, b.par], ALU.mult, "v_am")

            def weights_lo(b):
                after(e, "a_ah", b)
                after(e, "t_av", b + -1)
                tt(al[:, :, :], am[:, :, :], f32(ah[:, :, :]), ALU.subtract, "v_al")

            def stats2(b, bank=X0):
                after(e, "t_x1", b)
                for j in range(TILES):
                    q = e.bn_stats(st2[:, j, :], bank[:, j * P:(j + 1) * P])
                q.then_inc(s["v_st2"], 1)
                settled(e, "v_st2", b)
                for j in range(TILES):
                    q = e.bn_aggr(mv2[:, j, :], st2[:, j, :])
                q.then_inc(s["v_agg2"], 1)
                after(e, "v_agg2", b)
                after(e, "p_rs2", b + -1)
                e.tensor_scalar(ve2[:, :], mv2[:, :, 1], EPS, None, ALU.add).then_inc(s["v_rs2"], 1)

            def normalize2(b, bank=X0):
                after(e, "p_rs2", b)
                after(e, "t_x2", b + -1)
                for j in range(TILES):
                    q = e.tensor_scalar(xn2[:, j, :], bank[:, j * P:(j + 1) * P], mv2[:, j, 0:1],
                                        rs2[:, j:j + 1], ALU.subtract, ALU.mult)
                q.then_inc(s["v_norm2"], 1)

            def conv2_sum(b):
                after(e, "t_conv2", b)
                after(e, "a_c", b + -1)
                e.scalar_tensor_tensor(out=ct[:, :], in0=C2[:, :], scalar=s2[:, 0:1],
                                       in1=xnf[:, b.par], op0=ALU.mult, op1=ALU.add
                                       ).then_inc(s["v_ct"], 1)

            def conv2_lo(b):
                after(e, "a_c", b)
                after(e, "t_n", b + -1)
                tt(cl[:, :], cf[:, :], f32(chh[:, :]), ALU.subtract, "v_cl")

            def choose(b):
                after(e, "t_gate", b)
                sc = X2[:, :].rearrange("p (j n) -> p j n", j=TILES)[:, :, 0:EXPERTS]
                tt(gs[:, :, :], sc, bgate[:, :].rearrange("p (j n) -> p j n", j=TILES), ALU.add, "v_gs")

            def choose_b(b):
                after(e, "v_gs", b)
                shape = [P, TILES, EXPERTS, EXPERTS]
                other = gs[:, :, :].unsqueeze(2).broadcast_to(shape)
                own = gs[:, :, :].unsqueeze(3).broadcast_to(shape)
                tt(cmp_[:, :, :, :], other, own, ALU.is_gt, "v_cmp")
                tt(ceq[:, :, :, :], other, own, ALU.is_equal, "v_ceq")
                after(e, "v_ceq", b)
                tt(ceq[:, :, :, :], ceq[:, :, :, :],
                   earlier[:, :, :].unsqueeze(1).broadcast_to(shape), ALU.mult, "v_sum")
                e.wait_ge(s["v_sum"], 2 * b.index + 1)
                after(e, "v_cmp", b)
                tt(cmp_[:, :, :, :], cmp_[:, :, :, :], ceq[:, :, :, :], ALU.add, "v_sum")
                e.wait_ge(s["v_sum"], 2 * b.index + 2)
                e.tensor_reduce(rank[:, :, :], cmp_[:, :, :, :], AX.X, ALU.add).then_inc(s["v_rank"], 1)
                after(e, "v_rank", b)
                e.tensor_scalar(mask[:, :], rank[:, :, :].rearrange("p j n -> p (j n)"), 1.5, None,
                                ALU.is_lt).then_inc(s["v_mask"], 1)

            def mask_out(b):
                after(e, "t_mask", b)
                if b.known(1, BLOCKS):
                    e.wait_ge(s["st_mk"], 16 * b.index)
                e.tensor_copy(maskT[:, :], X2[:, :].bitcast(BF16)[0:TILES * EXPERTS, 0:P]
                              ).then_inc(s["v_mT"], 1)

            def body(b):
                prev, nxt = b.known(1, BLOCKS + 1), b.known(0, BLOCKS - 1)
                old = b.known(2, BLOCKS)
                if nxt:
                    stats(b + 1)
                if prev:
                    gru_a(b + -1)
                if nxt:
                    normalize(b + 1)
                if old:
                    choose(b + -2)
                    choose_b(b + -2)
                nmp_lo(b)
                if prev:
                    gru_d(b + -1)
                if nxt:
                    norm_lo(b + 1)
                if old:
                    mask_out(b + -2)
                if prev:
                    gru_b(b + -1)
                if nxt:
                    messages(b + 1)
                    factors(b + 1)
                    conv1_lo(b + 1)
                if prev:
                    stats2(b + -1)
                if nxt:
                    messages_lo(b + 1)
                if prev:
                    normalize2(b + -1)
                conv2_sum(b)
                if nxt:
                    weights(b + 1)
                conv2_lo(b)
                if nxt:
                    weights_lo(b + 1)

            stats(Block(0, 0))
            e.wait_ge(s["ld_c"], 48)
            e.tensor_scalar(bnv[:, 0:1], vec[:, BN1_V:BN1_V + 1], EPS, None, ALU.add).then_inc(s["k_bn"], 1)
            e.tensor_scalar(bnv[:, 1:2], vec[:, BN2_V:BN2_V + 1], EPS, None, ALU.add).then_inc(s["k_bn"], 1)
            for n, at_b in enumerate((BHH_R, BHH_Z)):
                tt(hb[:, n:n + 1], vec[:, BIH_R + n:BIH_R + n + 1], vec[:, at_b:at_b + 1], ALU.add, "k_hb")
            e.tensor_copy(hb[:, 2:3], vec[:, BHH_N:BHH_N + 1]).then_inc(s["k_hb"], 1)
            e.wait_ge(s["ld_id"], 16)
            e.tensor_copy(identb[:, :], ident[:, :]).then_inc(s["k_id"], 1)
            e.wait_ge(s["k_hb"], 3)
            e.tensor_scalar(hb[:, :], hb[:, :], 0.5, None, ALU.mult).then_inc(s["k_hb"], 1)
            normalize(Block(0, 0))
            e.wait_ge(s["k_w1"], 1)
            tt(w1c_lo[:, :], raw_w1c, f32(w1c_hi[:, :]), ALU.subtract, "k_sp_dve")
            e.wait_ge(s["k_bnp"], 1)
            tt(s1[:, :], vec[:, BN1_G:BN1_G + 1], bnr[:, 0:1], ALU.mult, "k_bnr")
            tt(s2[:, :], vec[:, BN2_G:BN2_G + 1], bnr[:, 1:2], ALU.mult, "k_bnr")
            e.wait_ge(s["k_bnr"], 2)
            tt(bnt[:, 0:1], vec[:, BN1_M:BN1_M + 1], s1[:, :], ALU.mult, "k_bnr")
            tt(bnt[:, 1:2], vec[:, BN2_M:BN2_M + 1], s2[:, :], ALU.mult, "k_bnr")
            e.wait_ge(s["k_bnr"], 4)
            tt(o1[:, :], vec[:, BN1_B:BN1_B + 1], bnt[:, 0:1], ALU.subtract, "k_bno")
            tt(o2[:, :], vec[:, BN2_B:BN2_B + 1], bnt[:, 1:2], ALU.subtract, "k_bno")
            norm_lo(Block(0, 0))
            e.wait_ge(s["k_ones"], 1)
            messages(Block(0, 0))
            factors(Block(0, 0))
            conv1_lo(Block(0, 0))
            e.wait_ge(s["k_g"], 1)
            tt(w2c_lo[:, :, :].rearrange("p k n -> p (k n)"), raw_w2c,
               f32(w2c_hi[:, :, :].rearrange("p k n -> p (k n)")), ALU.subtract, "k_sp_dve")
            messages_lo(Block(0, 0))
            weights(Block(0, 0))
            weights_lo(Block(0, 0))
            e.wait_ge(s["k_g"], 2)
            tt(wg_lo[:, :, :].rearrange("p k n -> p (k n)"), raw_wg,
               f32(wg_hi[:, :, :].rearrange("p k n -> p (k n)")), ALU.subtract, "k_sp_dve")
            e.wait_ge(s["ld_c2"], 16 * 3)
            for n in range(3):
                body(Block(0, n))
            pairs_loop(e, 3, (BLOCKS - 4) // 2, body)
            last = Block(0, BLOCKS - 1)
            body(last)

            def hidden_lo(b, x, chunks=range(CH)):
                p, n = x % 2, EXPERTS * b.index + x
                for c in chunks:
                    part = slice(c * BLOCK, (c + 1) * BLOCK)
                    e.wait_ge(s["f_hh"], CH * n + c + 1)
                    if c == 0 and (x >= 2 or b.known(1, BLOCKS)):
                        e.wait_ge(s["f_down"], n - 1)
                    tt(hl[p][:, part], hf[p][:, part], f32(hh[p][:, part]), ALU.subtract, "f_hl")

            def masked(b, x):
                p, n = x % 2, EXPERTS * b.index + x
                e.wait_ge(s["f_down"], n + 1)
                if x == 0:
                    loaded(e, "f_mk", b)
                e.scalar_tensor_tensor(out=ym[p], in0=down[p][:, :],
                                       scalar=vec[:, B2_AT + x:B2_AT + x + 1],
                                       in1=maskb[b.par][:, x, :], op0=ALU.add, op1=ALU.mult
                                       ).then_inc(s["f_ym"], 1)

            def add(b, x):
                p, n = x % 2, EXPERTS * b.index + x
                e.wait_ge(s["f_ym"], n + 1)
                if x == 0:
                    loaded(e, "f_x1", b)
                else:
                    e.wait_ge(s["f_acc"], n)
                tt(x1r[b.par], x1r[b.par], ym[p], ALU.add, "f_acc")

            def turn(b):
                at = b.index if isinstance(b.k, int) else None
                for x in range(EXPERTS):
                    if (at, x) == (0, 2):
                        stats2(last, X1)
                    if (at, x) == (0, 3):
                        normalize2(last, X1)
                    if (at, x) == (0, 5):
                        choose(last + -1)
                    if (at, x) == (1, 0):
                        choose_b(last + -1)
                    if (at, x) == (1, 3):
                        mask_out(last + -1)
                    if (at, x) == (1, 6):
                        choose(last)
                    if (at, x) == (2, 0):
                        choose_b(last)
                    if (at, x) == (2, 4):
                        mask_out(last)
                    ahead = (b, x + 1) if x + 1 < EXPERTS else (b + 1, 0)
                    more = x + 1 < EXPERTS or b.known(0, BLOCKS - 1)
                    if more:
                        hidden_lo(*ahead, range(CH - 1))
                    masked(b, x)
                    if more:
                        hidden_lo(*ahead, [CH - 1])
                    add(b, x)

            gru_a(last)
            gru_d(last)
            hidden_lo(Block(0, 0), 0)
            gru_b(last)
            for n in range(3):
                turn(Block(0, n))
            pairs_loop(e, 3, (BLOCKS - 4) // 2, turn)
            turn(Block(0, BLOCKS - 1))

        @blk.tensor
        def _(e):
            def mm3(o, w_hi, w_lo, m_hi, m_lo, first, end):
                e.matmul(o, w_hi, m_hi, start=first, stop=False)
                e.matmul(o, w_hi, m_lo, start=False, stop=False)
                return e.matmul(o, w_lo, m_hi, start=False, stop=end)

            def conv2(b, lo, hi):
                ps = C2[:, :].rearrange("p (g n) -> p g n", g=GP)
                if lo == 0:
                    after(e, "v_h1l", b)
                    after(e, "a_h1h", b)
                    after(e, "v_ct", b + -1)
                for k in range(lo, hi):
                    m = mm3(ps, w2c_hi[:, k, :], w2c_lo[:, k, :], h1h[:, b.par, :, k:k + NODES],
                            h1l[:, b.par, :, k:k + NODES], k == 0, k == TAPS - 1)
                if hi == TAPS:
                    m.then_inc(s["t_conv2"], 1)

            def message_pass(b):
                after(e, "v_ml", b)
                after(e, "v_al", b)
                after(e, "a_u", b + -1)
                for g in range(GP):
                    for m in range(MB):
                        j = g * MB + m
                        q = mm3(PH[:, g * NODES:(g + 1) * NODES], mh[:, j * P:(j + 1) * P],
                                ml[:, j * P:(j + 1) * P], ah[:, j, :], al[:, j, :], m == 0, m == MB - 1)
                q.then_inc(s["t_av"], 1)

            def turn_in(b):
                after(e, "v_norm", b)
                for j in range(TILES):
                    q = e.transpose(X0[:, j * P:(j + 1) * P], xn[:, j, :], ident[:, :])
                q.then_inc(s["t_in"], 1)

            def conv1(b):
                after(e, "a_xnh", b)
                after(e, "v_xnl", b)
                mm3(X1[:, :], w1c_hi[:, :], w1c_lo[:, :], xnh[:, b.par], xnl[:, b.par], True, True
                    ).then_inc(s["t_conv1"], 1)

            def messages(b):
                after(e, "a_xnf", b)
                after(e, "a_rt", b + -2)
                after(e, "v_mT", b + -3)
                half = TILES // 2
                for j in range(TILES):
                    bank, at = (PR, X2)[j // half], j % half * MSG
                    q = e.matmul(bank[:, at:at + MSG], xnf[:, b.par, j * P:(j + 1) * P],
                                 wmsg[:, :], start=True, stop=True)
                q.then_inc(s["t_msg"], 1)

            def turn_factors(b):
                after(e, "v_fac", b)
                after(e, "a_h1", b)
                for j in range(TILES):
                    q = e.transpose(X1[:, j * P:(j + 1) * P], f32(fac[:, j, :]), ident[:, :])
                q.then_inc(s["t_fac"], 1)

            def distances(b):
                after(e, "a_fr", b)
                after(e, "a_zt", b + -2)
                after(e, "v_w", b + -2)
                for g, ps in enumerate((PZ, PI)):
                    for m in range(MB):
                        j = g * MB + m
                        q = e.matmul(ps[:, m * NODES:(m + 1) * NODES], fl[:, j * P:(j + 1) * P],
                                     fr[:, g * NODES:(g + 1) * NODES], start=True, stop=True)
                    q.then_inc(s[f"t_dist{g}"], 1)

            def turn_x1(b, bank=X0):
                after(e, "v_x1", b)
                after(e, "v_xnl", b + 2)
                after(e, "a_xnf", b + 2)
                for j in range(TILES):
                    q = e.transpose(bank[:, j * P:(j + 1) * P], x1[:, j * P:(j + 1) * P], ident[:, :])
                q.then_inc(s["t_x1"], 1)

            def turn_x2(b):
                after(e, "v_norm2", b)
                after(e, "a_fr", b + 2)
                for j in range(TILES):
                    q = e.transpose(X1[:, j * P:(j + 1) * P], xn2[:, j, :], ident[:, :])
                q.then_inc(s["t_x2"], 1)

            def gate(b):
                after(e, "a_x2", b)
                after(e, "v_mt", b + 1)
                for j in range(TILES):
                    q = e.matmul(X2[:, j * P:(j + 1) * P], x2c[:, j * P:(j + 1) * P], wgate[:, :],
                                 start=True, stop=True)
                q.then_inc(s["t_gate"], 1)

            def gru(b):
                end = isinstance(b.k, int) and b.index == BLOCKS - 1
                xh, xl = xnh[:, b.par], xnl[:, b.par]

                def part(ps, w, g, m_hi, m_lo, first, last):
                    return mm3(ps[:, :], wg_hi[:, w, g * D:(g + 1) * D], wg_lo[:, w, g * D:(g + 1) * D],
                               m_hi, m_lo, first, last)

                if isinstance(b.k, int) and b.index == 0:
                    e.wait_ge(s["k_sp_dve"], 3)
                    e.wait_ge(s["k_g"], 2)
                if end:
                    after(e, "a_rt", b + -1)
                    after(e, "a_zt", b + -1)
                    after(e, "v_w", b + -1)
                after(e, "v_mt", b + 1)
                after(e, "a_e1", b + 1)
                after(e, "a_nh", b)
                after(e, "v_nl", b)
                part(PH, 2, 2, xh, xl, True, True).then_inc(s["t_gh"], 1)
                part(PR, 2, 0, xh, xl, True, False)
                part(PZ, 2, 1, xh, xl, True, False)
                if b.known(1, BLOCKS):
                    turn_x2(b + -1)
                part(PR, 1, 0, nh[:, :], nl[:, :], False, False)
                part(PZ, 1, 1, nh[:, :], nl[:, :], False, False)
                part(PI, 1, 2, nh[:, :], nl[:, :], True, False)
                after(e, "a_ch", b)
                after(e, "v_cl", b)
                part(PR, 0, 0, chh[:, :], cl[:, :], False, True).then_inc(s["t_r"], 1)
                part(PZ, 0, 1, chh[:, :], cl[:, :], False, True).then_inc(s["t_z"], 1)
                part(PI, 0, 2, chh[:, :], cl[:, :], False, True).then_inc(s["t_n"], 1)

            def turn_mask(b):
                after(e, "v_mask", b)
                after(e, "v_gs", b)
                e.transpose(X2[:, :].bitcast(BF16)[0:TILES * EXPERTS, 0:P], mask[:, :], identb[:, :]
                            ).then_inc(s["t_mask"], 1)

            def body(b):
                prev, nxt = b.known(1, BLOCKS + 1), b.known(0, BLOCKS - 1)
                old = b.known(2, BLOCKS)
                if old:
                    gate(b + -2)
                conv2(b, 0, 4)
                message_pass(b)
                conv2(b, 4, 6)
                if nxt:
                    turn_in(b + 1)
                if old:
                    turn_mask(b + -2)
                conv2(b, 6, 10)
                if nxt:
                    messages(b + 1)
                    conv1(b + 1)
                conv2(b, 10, 12)
                if prev:
                    turn_x1(b + -1)
                conv2(b, 12, 13)
                if nxt:
                    turn_factors(b + 1)
                conv2(b, 13, 15)
                if nxt:
                    distances(b + 1)
                conv2(b, 15, TAPS)
                gru(b)

            e.wait_ge(s["ld_id"], 16)
            turn_in(Block(0, 0))
            e.wait_ge(s["ld_c"], 48)
            messages(Block(0, 0))
            e.wait_ge(s["k_sp_dve"], 1)
            conv1(Block(0, 0))
            turn_factors(Block(0, 0))
            distances(Block(0, 0))
            e.wait_ge(s["k_sp_dve"], 2)
            e.wait_ge(s["k_g"], 1)
            body(Block(0, 0))
            e.wait_ge(s["ld_c2"], 16 * 3)
            e.wait_ge(s["k_id"], 1)
            body(Block(0, 1))
            body(Block(0, 2))
            pairs_loop(e, 3, (BLOCKS - 4) // 2, body)
            last = Block(0, BLOCKS - 1)
            body(last)

            def up_proj(b, x):
                p, n = x % 2, EXPERTS * b.index + x
                if x == 0:
                    e.wait_ge(s["f_qh"], b.index + 1)
                    e.wait_ge(s["f_ql"], b.index + 1)
                if x >= 2 or b.known(1, BLOCKS):
                    e.wait_ge(s["f_h"], CH * (n - 1))
                for c in range(CH):
                    mm3(up[p][c][:, :], wu_hi[:, x, c * P:(c + 1) * P], wu_lo[:, x, c * P:(c + 1) * P],
                        qh[b.par], ql[b.par], True, True).then_inc(s["f_up"], 1)

            def down_proj(b, x):
                p, n = x % 2, EXPERTS * b.index + x
                if x >= 2 or b.known(1, BLOCKS):
                    e.wait_ge(s["f_ym"], n - 1)
                for c in range(CH):
                    e.wait_ge(s["f_hl"], CH * n + c + 1)
                    q = mm3(down[p][:, :], wd_hi[:, x, c, :], wd_lo[:, x, c, :],
                            hh[p][:, c * BLOCK:(c + 1) * BLOCK], hl[p][:, c * BLOCK:(c + 1) * BLOCK],
                            c == 0, c == CH - 1)
                q.then_inc(s["f_down"], 1)

            def turn(b):
                at = b.index if isinstance(b.k, int) else None
                for x in range(EXPERTS):
                    if x + 1 < EXPERTS:
                        up_proj(b, x + 1)
                    elif b.known(0, BLOCKS - 1):
                        up_proj(b + 1, 0)
                    if (at, x) == (0, 1):
                        turn_x1(last, X1)
                    if (at, x) == (0, 3):
                        gate(last + -1)
                    if (at, x) == (0, 5):
                        turn_x2(last)
                    if (at, x) == (1, 2):
                        turn_mask(last + -1)
                    if (at, x) == (1, 4):
                        after(e, "v_mT", last + -1)
                        gate(last)
                    if (at, x) == (2, 3):
                        turn_mask(last)
                    down_proj(b, x)

            e.wait_ge(s["k_ff"], 4)
            after(e, "a_rt", last)
            after(e, "a_zt", last)
            up_proj(Block(0, 0), 0)
            after(e, "v_w", last)
            after(e, "a_u", last)
            for n in range(3):
                turn(Block(0, n))
            pairs_loop(e, 3, (BLOCKS - 4) // 2, turn)
            turn(Block(0, BLOCKS - 1))


def kernel(**inputs):
    import numpy as np
    import concourse.bacc as bacc
    from concourse.bass_utils import run_bass_kernel_spmd as run

    v = {k: np.asarray(x) for k, x in inputs.items()}
    gnn = lambda n: v["L0_gnn_" + n]
    ffn = lambda n: v["L0_ffn_" + n]
    tokens = GRAPHS * NODES
    w_ih, w_hh = gnn("w_ih"), gnn("w_hh")
    wgate = np.zeros((D, P), np.float32)
    wgate[:, :EXPERTS] = ffn("Wg")
    cols = [gnn(f"bn{n}_{c}") for n in (1, 2) for c in "gbmv"]
    cols += [gnn(w)[n * D:(n + 1) * D] for w in ("b_ih", "b_hh") for n in range(3)]
    cols += list(ffn("b1").reshape(EXPERTS * CH, P)) + list(ffn("b2"))
    arrays = {
        "x": v["x"].reshape(tokens, D),
        "xT": v["x"].reshape(tokens, D).T,
        "adjT": v["adj"].transpose(0, 2, 1).reshape(tokens, NODES),
        "conv1": gnn("conv1_w")[:, :, 0].T,
        "conv2": gnn("conv2_w").transpose(1, 2, 0).reshape(D, TAPS * D),
        "wgru": np.concatenate([w_ih[:, :D].T, w_ih[:, D:].T, w_hh.T], axis=1),
        "wmsg": np.concatenate([gnn("w_msg").T, gnn("w_se").T], axis=1),
        "wgate": wgate,
        "wup": ffn("W1").transpose(1, 0, 2).reshape(D, EXPERTS * HID),
        "wdown": ffn("W2").reshape(EXPERTS, CH, P, D).transpose(2, 0, 1, 3).reshape(P, -1),
        "vec": np.stack(cols, axis=1),
        "bmsg": np.broadcast_to(np.concatenate([gnn("b_msg"), gnn("b_se")]), (P, TILES // 2, MSG)),
        "bgate": np.broadcast_to(np.tile(ffn("bg"), TILES), (P, TILES * EXPERTS)),
        "ident": np.eye(P, dtype=np.float32),
        "earlier": np.broadcast_to(np.tril(np.ones((EXPERTS, EXPERTS), np.float32), -1),
                                   (P, EXPERTS, EXPERTS)),
    }
    arrays = {k: np.ascontiguousarray(x) for k, x in arrays.items()}
    nc = bacc.Bacc("TRN2", target_bir_lowering=False, num_devices=1)
    aps = {k: nc.dram_tensor(f"in_{k}", x.shape, mybir.dt.from_np(x.dtype), kind="ExternalInput").ap()
           for k, x in arrays.items()}
    out = nc.dram_tensor("outT", [P, tokens], F32, kind="ExternalOutput").ap()
    build(nc, aps, out)
    r = run(nc, [{f"in_{k}": x for k, x in arrays.items()}], core_ids=[0])
    return np.ascontiguousarray(r.results[0]["outT"].T).reshape(GRAPHS, NODES, D)
```

```python
from contextlib import ExitStack

import concourse.bass as bass
from concourse import mybir

F32 = mybir.dt.float32
F32R = mybir.dt.float32r
U32 = mybir.dt.uint32
I32 = mybir.dt.int32
BF16 = mybir.dt.bfloat16
ALU = mybir.AluOpType
ACT = mybir.ActivationFunctionType
AX = mybir.AxisListType

P = 128
GRAPHS, NODES, D = 32, 256, 128
GP = 2
BLOCK = GP * NODES
TILES = BLOCK // P
MB = NODES // P
BLOCKS = GRAPHS // GP
TAPS, PAD = 17, 8
WIDE = NODES + 2 * PAD
EXPERTS, HID = 8, 256
CH = HID // P
EPS = 1e-5
COORDS = 3
MSG = D + COORDS
ONCE, TWICE, FOUR = COORDS, 2 * COORDS, 4 * COORDS
FACTORS = FOUR + 4
RIGHT = 32

(BN1_G, BN1_B, BN1_M, BN1_V, BN2_G, BN2_B, BN2_M, BN2_V, BIH_R, BIH_Z, BIH_N, BHH_R, BHH_Z,
 BHH_N) = range(14)
B1_AT = 14
PICK = CH + 1
NVEC = B1_AT + EXPERTS * PICK

TOKENS = GRAPHS * NODES
CHOICES = 2
ROW = D + 1
REGION = TOKENS + BLOCK
FULL = CHOICES * TOKENS // BLOCK
SLOTS = FULL + EXPERTS
LIST_ROWS = EXPERTS * REGION + (SLOTS - FULL) * BLOCK
RESULT_ROWS = CHOICES * TOKENS + SLOTS * BLOCK
STEPS = TOKENS // BLOCK
CHUNK = 2 * BLOCK
CHUNKS = TOKENS // CHUNK


class Block:
    STEP = 2

    def __init__(self, k, off):
        self.k, self.off = k, off

    def __add__(self, n):
        return type(self)(self.k, self.off + n)

    @property
    def index(self):
        return self.STEP * self.k + self.off

    @property
    def par(self):
        return self.off % 2

    @property
    def half(self):
        return self.STEP // 2 * self.k + self.off // 2

    def known(self, low, high):
        return not isinstance(self.k, int) or low <= self.index < high


class Slot(Block):
    STEP = 4

    @property
    def quad(self):
        return self.off % 4


def build(nc, a, out):
    ctx = ExitStack()
    with ctx:
        def sb(name, shape, dt=F32):
            return ctx.enter_context(nc.sbuf_tensor(name, shape, dt))

        def sem(name):
            return ctx.enter_context(nc.semaphore(name))

        w2c_hi = sb("w2c_hi", [P, TAPS, D], F32R)
        w2c_lo = sb("w2c_lo", [P, TAPS, D], F32R)
        w1c_hi = sb("w1c_hi", [P, D], F32R)
        w1c_lo = sb("w1c_lo", [P, D], F32R)
        wg_hi = sb("wgru_hi", [P, 3, 3 * D], F32R)
        wg_lo = sb("wgru_lo", [P, 3, 3 * D], F32R)
        wmsg = sb("wmsg", [P, MSG])
        wgate = sb("wgate", [P, P])
        wu = sb("wup", [P, EXPERTS, 2, HID], F32R)
        wd = sb("wdown", [P, EXPERTS, 2, CH * D], F32R)
        vec = sb("vec", [P, NVEC])
        bmsg = sb("bmsg", [P, TILES // 2, MSG])
        before = sb("before", [P, P], BF16)
        ones = sb("ones", [P, P], BF16)
        before_f = sb("before_f", [P, P])
        regbase = sb("regbase", [P, EXPERTS])
        steps = sb("steps", [1, STEPS])
        slotnum = sb("slotnum", [1, SLOTS])
        ids = sb("ids", [P, 2, CHOICES, TILES])
        bgate = sb("bgate", [P, TILES * EXPERTS])
        ident = sb("ident", [P, P])
        earlier = sb("earlier", [P, EXPERTS, EXPERTS])
        halfpow = sb("halfpow", [P, 8])
        bnv = sb("bnv", [P, 2])
        bnr = sb("bnr", [P, 2])
        bnt = sb("bnt", [P, 2])
        spare = sb("spare", [P, 1])
        spare_p = sb("spare_p", [P, 1])
        spare_a = sb("spare_a", [P, 1])
        s1 = sb("s1", [P, 1])
        o1 = sb("o1", [P, 1])
        s2 = sb("s2", [P, 1])
        o2 = sb("o2", [P, 1])
        hb = sb("hb", [P, 3])
        STAGE = TAPS * D + 2 * EXPERTS * HID + 9 * D + D
        stage = sb("stage", [P, STAGE])
        at = [0]

        def view(n, dt=F32):
            lo = at[0]
            at[0] += n
            v = stage[:, lo:lo + n]
            return v if dt is F32 else v.bitcast(dt)

        raw_w2c = view(TAPS * D)
        raw_w1c = view(D)
        raw_wg = view(9 * D)
        raw_wu = view(EXPERTS * HID)
        raw_wd = view(EXPERTS * HID)
        at[0] = 0
        rows = view(2 * CHOICES * TILES * ROW).rearrange("p (q c j d) -> p q c j d", q=2, c=CHOICES,
                                                         j=TILES)
        rows_end = at[0]
        assert rows_end <= TAPS * D
        at[0] = TAPS * D + D
        xr = [view(TILES * ROW).rearrange("p (j d) -> p j d", j=TILES) for _ in range(2)]
        last_y = [[view(CHUNK) for _ in range(CHOICES)] for _ in range(2)]
        assert at[0] <= STAGE

        xt = sb("xtok", [P, 2, TILES, D])
        adj = sb("adj", [P, 2, TILES, NODES])
        xT = sb("xT", [P, 2, BLOCK])
        st = sb("st", [P, TILES, 6])
        mv = sb("mv", [P, TILES, 2])
        ve = sb("ve", [P, TILES])
        rs = sb("rs", [P, TILES])
        st2 = sb("st2", [P, TILES, 6])
        mv2 = sb("mv2", [P, TILES, 2])
        ve2 = sb("ve2", [P, TILES])
        rs2 = sb("rs2", [P, TILES])
        xn = sb("xn", [P, TILES, D])
        xnf = sb("xnT", [P, 2, BLOCK])
        xnh = sb("xnT_hi", [P, 2, BLOCK], F32R)
        xnl = sb("xnT_lo", [P, 2, BLOCK], F32R)
        h1f = sb("h1", [P, GP, NODES])
        h1h = sb("h1_hi", [P, 2, GP, WIDE], F32R)
        h1l = sb("h1_lo", [P, 2, GP, WIDE], F32R)
        sq3 = sb("sq3", [P, TILES, COORDS])
        sq = sb("sq", [P, TILES, 1])
        fac = sb("factors", [P, TILES, P], F32R)
        fl = sb("factors_left", [FACTORS, BLOCK], F32R)
        fr = sb("factors_right", [FACTORS, BLOCK], F32R)
        am = sb("am", [P, TILES, NODES])
        ah = sb("a_hi", [P, TILES, NODES], F32R)
        al = sb("a_lo", [P, TILES, NODES], F32R)
        mt = sb("mt", [P, TILES, MSG])
        mf = sb("msg", [P, TILES * D])
        mh = sb("msg_hi", [P, BLOCK], F32R)
        ml = sb("msg_lo", [P, BLOCK], F32R)
        nh = sb("nmp_hi", [P, BLOCK], F32R)
        nl = sb("nmp_lo", [P, BLOCK], F32R)
        ct = sb("ct", [P, BLOCK])
        cf = sb("xconv", [P, BLOCK])
        chh = sb("xconv_hi", [P, BLOCK], F32R)
        cl = sb("xconv_lo", [P, BLOCK], F32R)
        rt = sb("rt", [P, BLOCK])
        zt = sb("zt", [P, BLOCK])
        uu = sb("uu", [P, BLOCK])
        vv = sb("vv", [P, BLOCK])
        nn = sb("nn", [P, BLOCK])
        dd = sb("dd", [P, BLOCK])
        x1 = sb("x1T", [P, BLOCK])
        x1t = sb("x1tok", [P, BLOCK])
        x2c = sb("xn2T", [P, BLOCK])
        gs = sb("gs", [P, TILES, EXPERTS])
        cmp_ = sb("cmp", [P, TILES, EXPERTS, EXPERTS])
        ceq = sb("ceq", [P, TILES, EXPERTS, EXPERTS])
        rank = sb("rank", [P, TILES, EXPERTS])
        mask = sb("mask", [P, TILES + 1, EXPERTS], BF16)
        base = sb("base", [P, EXPERTS])
        pos = sb("pos", [P, TILES, EXPERTS])
        sel = sb("sel", [P, CHOICES, TILES, EXPERTS])
        row_f = sb("row_f", [P, CHOICES, TILES])
        row_at = sb("row_at", [P, 2, CHOICES, TILES], U32)

        length = sb("length", [1, EXPERTS])
        more = sb("more", [1, EXPERTS, STEPS])
        used = sb("used", [1, EXPERTS])
        usedm = sb("usedm", [1, EXPERTS, EXPERTS])
        first = sb("first", [1, EXPERTS])
        past = sb("past", [1, EXPERTS])
        ind = sb("ind", [1, SLOTS, EXPERTS])
        indn = sb("indn", [1, SLOTS, EXPERTS])
        whose = sb("whose", [1, SLOTS])
        gone = sb("gone", [1, SLOTS])
        start = sb("start", [1, SLOTS])
        start_i = sb("start_i", [1, SLOTS], I32)
        whose_i = sb("whose_i", [1, SLOTS], I32)
        end_i = sb("end_i", [1, EXPERTS], I32)
        b1s = sb("b1s", [P, 2, CH])
        b2s = sb("b2s", [P, 2, 1])
        goes = sb("goes", [P, 4, TILES])
        pad = sb("pad", [P, TILES])
        padbase = sb("padbase", [P, 1])
        result_at = sb("result_at", [P, 4, TILES], U32)

        hf = [am[:, :, :].rearrange("p t n -> p (t n)"),
              xnf[:, :, :].rearrange("p t n -> p (t n)")]
        hh = [ah[:, :, :].rearrange("p t n -> p (t n)"), al[:, :, :].rearrange("p t n -> p (t n)")]
        hl = [xnh[:, :, :].rearrange("p t n -> p (t n)"), xnl[:, :, :].rearrange("p t n -> p (t n)")]
        qh = [mh[:, :], nh[:, :]]
        ql = [ml[:, :], nl[:, :]]
        old = [adj[:, :, :, :].rearrange("p q j n -> p (q j n)"),
               xt[:, :, :, :].rearrange("p q j n -> p (q j n)"),
               xT[:, :, :].rearrange("p q n -> p (q n)"), stage[:, 0:CHOICES * CHUNK]]
        last_x = [t[:, n:n + BLOCK] for t in old for n in range(0, t.shape[1], BLOCK)]
        last_x += [mf[:, :], ct[:, :], cf[:, :], dd[:, :]]
        assert len(last_x) == BLOCKS
        yf = [rt[:, :], zt[:, :]]
        yt = [uu[:, :], vv[:, :]]
        wcur = [[t[:, q].rearrange("p g n -> p (g n)")[:, 0:2 * HID].rearrange("p (s n) -> p s n", s=2)
                 for q in range(2)] for t in (h1h, h1l)]

        banks = [ctx.enter_context(nc.psum_tensor(f"bank{n}", [P, BLOCK], F32)) for n in range(8)]
        X0, X1, X2, C2, PR, PZ, PI, PH = banks
        up = [[PR, PZ], [PI, PH]]
        turned = [X1, X2]

        d_x1 = nc.dram_tensor("kept_x1", [TOKENS, D], F32, kind="Internal").ap()
        d_list = nc.dram_tensor("lists", [LIST_ROWS, ROW], F32, kind="Internal").ap()
        d_y = nc.dram_tensor("results", [RESULT_ROWS, D], F32, kind="Internal").ap()

        def f32(ap):
            return ap.bitcast(F32)

        names = """ld_x0 ld_x1 ld_adj0 ld_adj1 ld_t0 ld_t1 ld_w2c ld_w1 ld_g ld_ff ld_c ld_c2 ld_id st_x1 st_pad st_pad_a
            k_init k_half k_sp_dve k_w1 k_g k_ff_hi k_ff k_bn k_bnp k_bnr k_bno k_hb k_id k_ones k_zero k_gelu p_settled
            v_st v_agg v_var v_norm p_rs v_rs2 p_rs2 v_st2 v_agg2
            t_in t_conv1 t_msg t_fac t_dist0 t_dist1 t_av t_x1 t_x2 t_conv2 t_gate t_gh t_r t_z t_n
            t_count a_x1t a_rows sc0 sc1 a_xnh a_xnf a_h1 a_h1h a_fl a_fr a_msg a_msgh a_e0 a_e1 a_ah a_nh a_c a_ch a_rt
            a_zt a_u a_nn a_x2 v_xnl v_h1l v_s_hi v_s_sq v_s_lo v_sq v_sq_hi v_sq_lo v_fac v_mt v_ml v_am v_al v_nl v_ct v_cl v_v v_w v_d
            v_e v_g v_x1 v_norm2 v_gs v_cmp v_ceq v_sum v_rank v_mask v_ids v_pos v_sel
            v_row v_place v_base k_tab k_table f_ld0 f_ld1 f_xt f_xh f_xl f_up f_h f_hh f_hl f_down
            f_y f_ty f_yt f_b1 f_b2 f_wu0 f_wu1 f_wd0 f_wd1 f_goes f_isp f_id f_pb f_sc0 f_sc1 l_x1 l_in0 l_in1 l_y l_sum l_out""".split()
        s = {n: sem(n) for n in names}

        def after(e, name, b):
            if b.known(0, BLOCKS):
                e.wait_ge(s[name], b.index + 1)

        def loaded(e, name, b):
            e.wait_ge(s[f"{name}{b.par}"], 16 * (b.half + 1))

        def tok(ap, b):
            return ap[:, bass.ds(b.index * BLOCK, BLOCK)]

        x_d = a["x"].rearrange("(b j p) d -> b p j d", j=TILES, p=P)
        x1_d = d_x1.rearrange("(b j p) d -> b p j d", j=TILES, p=P)
        adj_d = a["adjT"].rearrange("(b j p) n -> b p j n", j=TILES, p=P)

        def runs(ap):
            return ap.rearrange("(q r) d -> q (r d)", q=16)

        def pad_lists(e, experts, sig):
            e.wait_ge(s["k_table"], 1)
            for n in experts:
                end = e.value_load(end_i[0:1, n:n + 1], min_val=0, max_val=EXPERTS * REGION - BLOCK)
                e.dma_start(runs(d_list[bass.ds(end, BLOCK), :]), runs(a["padding"])
                            ).then_inc(s[sig], 16)

        def slots_loop(e, first, rounds, body):
            with e.Fori(0, rounds) as k:
                for n in range(Slot.STEP):
                    body(Slot(k, first + n))

        def slots(e, body):
            for n in range(2):
                body(Slot(0, n))
            slots_loop(e, 2, (SLOTS - 4) // 4, body)
            for n in range(SLOTS - 2, SLOTS):
                body(Slot(0, n))

        def seen(e, name, i, each=1):
            if i.known(0, SLOTS):
                e.wait_ge(s[name], each * (i.index + 1))

        blk = ctx.enter_context(nc.Block())

        def pairs_loop(e, first, rounds, body):
            with e.Fori(0, rounds) as k:
                body(Block(k, first))
                body(Block(k, first + 1))

        @blk.sync
        def _(e):
            def load_x(b):
                after(e, "v_norm", b + -2)
                e.dma_start(xt[:, b.par], x_d[b.index]).then_inc(s[f"ld_x{b.par}"], 16)

            def load_adj(b):
                after(e, "v_am", b + -2)
                e.dma_start(adj[:, b.par], adj_d[b.index]).then_inc(s[f"ld_adj{b.par}"], 16)

            def load_xT(b):
                after(e, "v_x1", b + -2)
                e.dma_start(xT[:, b.par], tok(a["xT"], b)).then_inc(s[f"ld_t{b.par}"], 16)

            def keep_x1(b):
                after(e, "a_x1t", b)
                e.dma_start(x1_d[b.index], x1t[:, :].rearrange("p (j d) -> p j d", j=TILES)
                            ).then_inc(s["st_x1"], 16)

            def body(b):
                if b.known(0, BLOCKS - 2):
                    load_x(b + 2)
                    load_adj(b + 2)
                if b.known(0, BLOCKS - 1):
                    load_xT(b + 1)
                if b.known(1, BLOCKS):
                    keep_x1(b + -1)

            load_x(Block(0, 0))
            e.dma_start(ident[:, :], a["ident"]).then_inc(s["ld_id"], 16)
            e.dma_start(raw_w1c, a["conv1"]).then_inc(s["ld_w1"], 16)
            e.dma_start(vec[:, :], a["vec"]).then_inc(s["ld_c"], 16)
            e.dma_start(wmsg[:, :], a["wmsg"]).then_inc(s["ld_c"], 16)
            e.dma_start(bmsg[:, :, :], a["bmsg"]).then_inc(s["ld_c"], 16)
            load_adj(Block(0, 0))
            e.dma_start(raw_w2c, a["conv2"]).then_inc(s["ld_w2c"], 16)
            load_x(Block(0, 1))
            e.dma_start(raw_wg, a["wgru"]).then_inc(s["ld_g"], 16)
            load_xT(Block(0, 0))
            load_adj(Block(0, 1))
            e.dma_start(wgate[:, :], a["wgate"]).then_inc(s["ld_c2"], 16)
            e.dma_start(bgate[:, :], a["bgate"]).then_inc(s["ld_c2"], 16)
            e.dma_start(earlier[:, :, :], a["earlier"]).then_inc(s["ld_c2"], 16)
            e.dma_start(before_f[:, :], a["before"]).then_inc(s["ld_c2"], 16)
            e.dma_start(regbase[:, :], a["regbase"]).then_inc(s["ld_c2"], 16)
            e.dma_start(steps[:, :], a["steps"]).then_inc(s["ld_c2"], 16)
            e.dma_start(slotnum[:, :], a["slotnum"]).then_inc(s["ld_c2"], 16)
            e.dma_start(ids[:, :, :, :], a["ids"]).then_inc(s["ld_c2"], 16)
            e.dma_start(raw_wu, a["wup"]).then_inc(s["ld_ff"], 16)
            e.dma_start(raw_wd, a["wdown"]).then_inc(s["ld_ff"], 16)
            for n in range(SLOTS - FULL):
                at_row = EXPERTS * REGION + n * BLOCK
                e.dma_start(runs(d_list[at_row:at_row + BLOCK, :]), runs(a["padding"])
                            ).then_inc(s["st_pad"], 16)

            body(Block(0, 0))
            body(Block(0, 1))
            pairs_loop(e, 2, (BLOCKS - 4) // 2, body)
            body(Block(0, BLOCKS - 2))
            body(Block(0, BLOCKS - 1))
            keep_x1(Block(0, BLOCKS - 1))

            def fetch(i):
                at_row = e.value_load(start_i[0:1, bass.ds(i.index, 1)], min_val=0,
                                      max_val=LIST_ROWS - BLOCK)
                seen(e, "f_xt", i + -2)
                seen(e, "f_goes", i + -2)
                e.dma_start(xr[i.par], d_list[bass.ds(at_row, BLOCK), :].rearrange(
                    "(j p) d -> p j d", p=P)).then_inc(s[f"f_ld{i.par}"], 16)

            def fetch_weights(i, which):
                x = e.value_load(whose_i[0:1, bass.ds(i.index, 1)], min_val=0, max_val=EXPERTS - 1)
                if which == 0:
                    seen(e, "f_up", i + -2, CH)
                else:
                    seen(e, "f_down", i + -2)
                name = ("f_wu", "f_wd")[which]
                e.dma_start(f32(wcur[which][i.par]).unsqueeze(1), f32((wu, wd)[which][:, bass.ds(x, 1)])
                            ).then_inc(s[f"{name}{i.par}"], 16)

            def fetch_all(i):
                fetch(i)
                if i.known(1, SLOTS):
                    fetch_weights(i, 0)
                if i.known(1, SLOTS):
                    fetch_weights(i + -1, 1)

            pad_lists(e, range(EXPERTS // 2), "st_pad")
            e.wait_ge(s["k_table"], 3)
            fetch_weights(Slot(0, 0), 0)
            e.wait_ge(s["st_pad"], 16 * (SLOTS - FULL + EXPERTS // 2))
            e.wait_ge(s["st_pad_a"], 16 * EXPERTS // 2)
            e.wait_ge(s["sc0"], 16 * CHOICES * TILES * BLOCKS // 2)
            e.wait_ge(s["sc1"], 16 * CHOICES * TILES * BLOCKS // 2)
            ya_c, yb_c = (t.rearrange("(c j p) d -> c p j d", p=P, j=CHUNK // P)
                          for t in (d_y[0:TOKENS, :], d_y[TOKENS:2 * TOKENS, :]))
            out_d = out.rearrange("(b j p) d -> b p j d", p=P, j=TILES)

            def tiles(ap):
                return ap.rearrange("p (j d) -> p j d", d=D)

            slots(e, fetch_all)
            fetch_weights(Slot(0, SLOTS - 1), 1)
            e.wait_ge(s["st_x1"], 16 * BLOCKS)
            for b in range(BLOCKS):
                e.dma_start(tiles(last_x[b]), x1_d[b]).then_inc(s["l_x1"], 16)

            def load_y(c):
                if c >= 2:
                    e.wait_ge(s["l_sum"], 2 * (c - 1))
                for t, y in zip((ya_c, yb_c), last_y[c % 2]):
                    e.dma_start(tiles(y), t[c]).then_inc(s[f"l_in{c % 2}"], 16)

            e.wait_ge(s["f_sc0"], 16 * TILES * SLOTS // 2)
            e.wait_ge(s["f_sc1"], 16 * TILES * SLOTS // 2)
            for c in range(2):
                load_y(c)
            for c in range(CHUNKS):
                for b in (2 * c, 2 * c + 1):
                    e.wait_ge(s["l_sum"], b + 1)
                    e.dma_start(out_d[b], tiles(last_x[b])).then_inc(s["l_out"], 16)
                if c + 2 < CHUNKS:
                    load_y(c + 2)
            e.wait_ge(s["l_out"], 16 * BLOCKS)

        @blk.gpsimd
        def _(e):
            e.memset(halfpow[:, :], -0.5).then_inc(s["k_half"], 1)
            e.wait_ge(s["k_half"], 1)

            def root(b):
                after(e, "v_var", b)
                after(e, "v_norm", b + -1)
                e.tensor_tensor(rs[:, :], ve[:, :], halfpow[:, 0:TILES], ALU.pow).then_inc(s["p_rs"], 1)

            def root2(b):
                after(e, "v_rs2", b)
                after(e, "v_norm2", b + -1)
                e.tensor_tensor(rs2[:, :], ve2[:, :], halfpow[:, 0:TILES], ALU.pow).then_inc(s["p_rs2"], 1)

            def body(b):
                first = isinstance(b.k, int) and b.index < PIECES
                if b.known(0, BLOCKS - 1):
                    root(b + 1)
                if first:
                    split_piece(b.index)
                if b.known(2, BLOCKS):
                    append(b + -2, 0)
                if b.known(1, BLOCKS + 1):
                    root2(b + -1)
                if b.known(2, BLOCKS):
                    append(b + -2, 1)

            def settled(e, name, n, done):
                if not (isinstance(done, int) and done == 0):
                    e.wait_ge(s["p_settled"], done)
                e.wait_ge(s[name], n)
                e.tensor_tensor(spare_p[:, :], halfpow[:, 0:1], halfpow[:, 0:1], ALU.add
                                ).then_inc(s["p_settled"], 1)

            def append(b, c):
                settled(e, ("v_place", "a_rows")[c], b.index + 1, CHOICES * b.index + c)
                for j in range(TILES):
                    e.indirect_dma_start(d_list, bass.IndirectOffsetOnAxis(row_at[:, b.par, c, j:j + 1], 0),
                                         rows[:, b.par, c, j, :], None).then_inc(s[f"sc{b.par}"], 16)

            PIECES = 2

            def split_piece(i):
                if i == 0:
                    e.wait_ge(s["ld_ff"], 32)
                for m, (raw, w) in enumerate(((raw_wu, wu), (raw_wd, wd))):
                    part = slice(i * EXPERTS // PIECES, (i + 1) * EXPERTS // PIECES)
                    r = raw.rearrange("p (e n) -> p e n", e=EXPERTS)[:, part]
                    e.tensor_copy(w[:, part, 0, :], r).then_inc(s["k_ff_hi"], 1)
                    e.wait_ge(s["k_ff_hi"], 2 * i + m + 1)
                    e.tensor_tensor(w[:, part, 1, :], r, f32(w[:, part, 0, :]),
                                    ALU.subtract).then_inc(s["k_ff"], 1)

            root(Block(0, 0))
            e.wait_ge(s["k_bn"], 2)
            e.tensor_tensor(bnr[:, :], bnv[:, :], halfpow[:, 0:2], ALU.pow).then_inc(s["k_bnp"], 1)
            e.memset(h1h[:, :, :, :].bitcast(F32), 0.0).then_inc(s["k_init"], 1)
            e.memset(h1l[:, :, :, :].bitcast(F32), 0.0).then_inc(s["k_init"], 1)
            for n in range(3):
                body(Block(0, n))
            pairs_loop(e, 3, (BLOCKS - 4) // 2, body)
            body(Block(0, BLOCKS - 1))

            last = Block(0, BLOCKS - 1)
            root2(last)
            append(last + -1, 0)
            append(last + -1, 1)
            append(last, 0)
            append(last, 1)

            def scatter(i):
                seen(e, "f_id", i)
                settled(e, "f_yt", i.index + 1, CHOICES * BLOCKS + i.index)
                for j in range(TILES):
                    e.indirect_dma_start(d_y, bass.IndirectOffsetOnAxis(result_at[:, i.quad, j:j + 1], 0),
                                         yt[i.par][:, j * P:(j + 1) * P], None
                                         ).then_inc(s[f"f_sc{i.par}"], 16)

            slots(e, scatter)

        @blk.scalar
        def _(e):
            def act(o, i, f, sig, **kw):
                return e.activation(o, i, f, **kw).then_inc(s[sig], 1)

            e.wait_ge(s["ld_w1"], 16)
            act(w1c_hi[:, :], raw_w1c, ACT.Copy, "k_w1")

            def gru(b):
                after(e, "t_gh", b)
                after(e, "v_v", b + -1)
                act(uu[:, :], PH[:, :], ACT.Identity, "a_u", scale=0.5, bias=hb[:, 2:3])
                after(e, "t_r", b)
                act(rt[:, :], PR[:, :], ACT.Tanh, "a_rt", scale=0.5, bias=hb[:, 0:1])
                after(e, "t_z", b)
                after(e, "v_e", b + -1)
                act(zt[:, :], PZ[:, :], ACT.Tanh, "a_zt", scale=0.5, bias=hb[:, 1:2])
                after(e, "v_w", b)
                after(e, "v_g", b + -1)
                act(nn[:, :], vv[:, :], ACT.Tanh, "a_nn", bias=vec[:, BIH_N:BIH_N + 1])

            def nmp_hi(b):
                after(e, "t_av", b)
                after(e, "t_n", b + -1)
                act(nh[:, :], PH[:, :], ACT.Copy, "a_nh")

            def norm_out(b):
                after(e, "t_in", b)
                after(e, "t_n", b + -2)
                after(e, "v_d", b + -2)
                act(xnh[:, b.par], X0[:, :], ACT.Copy, "a_xnh")
                act(xnf[:, b.par], X0[:, :], ACT.Copy, "a_xnf")

            def conv1_out(b):
                after(e, "t_conv1", b)
                if isinstance(b.k, int) and b.index == 0:
                    e.wait_ge(s["k_bno"], 2)
                    e.wait_ge(s["k_init"], 2)
                kw = dict(scale=s1[:, 0:1], bias=o1[:, 0:1])
                ps = X1[:, :].rearrange("p (g n) -> p g n", g=GP)
                after(e, "t_conv2", b + -2)
                act(h1h[:, b.par, :, PAD:PAD + NODES], ps, ACT.Relu, "a_h1h", **kw)
                after(e, "v_h1l", b + -1)
                act(h1f[:, :, :], ps, ACT.Relu, "a_h1", **kw)

            def factors(b):
                after(e, "t_fac", b)
                after(e, "t_dist1", b + -1)
                act(fl[:, :], X1[0:FACTORS, :], ACT.Copy, "a_fl")
                act(fr[:, :], X1[RIGHT:RIGHT + FACTORS, :], ACT.Copy, "a_fr")

            def messages(b):
                after(e, "v_mt", b)
                after(e, "t_av", b + -1)
                m = mt[:, :, 0:D]
                act(mh[:, :].rearrange("p (j d) -> p j d", j=TILES), m, ACT.Relu, "a_msgh")
                after(e, "v_ml", b + -1)
                act(mf[:, :].rearrange("p (j d) -> p j d", j=TILES), m, ACT.Relu, "a_msg")

            def weights_of(b):
                after(e, "v_al", b + -1)
                after(e, "a_ah", b + -1)
                for g, ps in enumerate((PZ, PI)):
                    after(e, f"t_dist{g}", b)
                    act(am[:, g * MB:(g + 1) * MB, :], ps[:, :].rearrange("p (m n) -> p m n", m=MB),
                        ACT.Exp, f"a_e{g}", scale=-1.0)

            def weights_hi(b):
                after(e, "v_am", b)
                after(e, "t_av", b + -1)
                act(ah[:, :, :], am[:, :, :], ACT.Copy, "a_ah")

            def x1_out(b):
                after(e, "v_st2", b)
                if b.known(1, BLOCKS):
                    e.wait_ge(s["st_x1"], 16 * b.index)
                act(x1t[:, :], X0[:, :], ACT.Copy, "a_x1t")

            def rows_out(b):
                after(e, "v_norm2", b)
                if b.known(2, BLOCKS):
                    e.wait_ge(s[f"sc{b.par}"], 16 * CHOICES * TILES * b.half)
                act(rows[:, b.par, 1, :, 0:D], rows[:, b.par, 0, :, 0:D], ACT.Copy, "a_rows")

            def norm2_out(b):
                after(e, "t_x2", b)
                after(e, "t_gate", b + -1)
                act(x2c[:, :], X1[:, :], ACT.Copy, "a_x2")

            def conv2_out(b):
                after(e, "v_ct", b)
                after(e, "t_n", b + -1)
                act(chh[:, :], ct[:, :], ACT.Relu, "a_ch", bias=o2[:, 0:1])
                after(e, "v_cl", b + -1)
                act(cf[:, :], ct[:, :], ACT.Relu, "a_c", bias=o2[:, 0:1])

            def body(b):
                prev, nxt = b.known(1, BLOCKS + 1), b.known(0, BLOCKS - 1)
                if prev:
                    gru(b + -1)
                nmp_hi(b)
                if nxt:
                    norm_out(b + 1)
                    conv1_out(b + 1)
                    messages(b + 1)
                    factors(b + 1)
                if prev:
                    x1_out(b + -1)
                if nxt:
                    weights_of(b + 1)
                conv2_out(b)
                if nxt:
                    weights_hi(b + 1)
                if prev:
                    norm2_out(b + -1)
                    rows_out(b + -1)

            norm_out(Block(0, 0))
            e.wait_ge(s["ld_w2c"], 16)
            act(w2c_hi[:, :, :].rearrange("p k n -> p (k n)"), raw_w2c, ACT.Copy, "k_g")
            conv1_out(Block(0, 0))
            messages(Block(0, 0))
            factors(Block(0, 0))
            weights_of(Block(0, 0))
            weights_hi(Block(0, 0))
            e.wait_ge(s["ld_g"], 16)
            act(wg_hi[:, :, :].rearrange("p k n -> p (k n)"), raw_wg, ACT.Copy, "k_g")
            for n in range(3):
                body(Block(0, n))
            pairs_loop(e, 3, (BLOCKS - 4) // 2, body)
            body(Block(0, BLOCKS - 1))

            last = Block(0, BLOCKS - 1)
            gru(last)
            x1_out(last)
            norm2_out(last)
            rows_out(last)

            def x_hi(i):
                seen(e, "f_xt", i)
                seen(e, "f_up", i + -2, CH)
                act(qh[i.par], X0[:, :], ACT.Copy, "f_xh")

            def hidden(i):
                for c in range(CH):
                    part = slice(c * BLOCK, (c + 1) * BLOCK)
                    if c == 0:
                        seen(e, "f_b1", i)
                        seen(e, "f_hl", i + -2, CH)
                    e.wait_ge(s["f_up"], CH * i.index + c + 1)
                    act(hf[i.par][:, part], up[i.par][c][:, :], ACT.Gelu, "f_h",
                        bias=b1s[:, i.par, c:c + 1])
                    if c == 0:
                        seen(e, "f_down", i + -2)
                    e.wait_ge(s["f_h"], CH * i.index + c + 1)
                    act(hh[i.par][:, part], hf[i.par][:, part], ACT.Copy, "f_hh")

            def y_out(i):
                seen(e, "f_b2", i)
                seen(e, "f_ty", i + -2)
                seen(e, "f_down", i)
                act(yf[i.par], C2[:, :], ACT.Identity, "f_y", bias=b2s[:, i.par, :])

            def turn(i):
                if i.known(0, SLOTS - 2):
                    x_hi(i + 2)
                if i.known(0, SLOTS - 1):
                    hidden(i + 1)
                y_out(i)

            pad_lists(e, range(EXPERTS // 2, EXPERTS), "st_pad_a")
            act(spare_a[:, :], halfpow[:, 0:1], ACT.Gelu, "k_gelu")
            x_hi(Slot(0, 0))
            x_hi(Slot(0, 1))
            hidden(Slot(0, 0))
            slots(e, turn)

        @blk.vector
        def _(e):
            def tt(o, i, j, op, sig):
                return e.tensor_tensor(o, i, j, op).then_inc(s[sig], 1)

            e.memset(f32(fac[:, :, :]), 1.0).then_inc(s["k_ones"], 1)

            def settled(e, name, b):
                after(e, name, b)
                e.memset(spare[:, :], 0.0)

            def stats(b):
                loaded(e, "ld_x", b)
                after(e, "v_agg", b + -1)
                for j in range(TILES):
                    q = e.bn_stats(st[:, j, :], xt[:, b.par, j, :])
                q.then_inc(s["v_st"], 1)
                settled(e, "v_st", b)
                for j in range(TILES):
                    q = e.bn_aggr(mv[:, j, :], st[:, j, :])
                q.then_inc(s["v_agg"], 1)
                after(e, "v_agg", b)
                after(e, "p_rs", b + -1)
                e.tensor_scalar(ve[:, :], mv[:, :, 1], EPS, None, ALU.add).then_inc(s["v_var"], 1)

            def normalize(b):
                after(e, "p_rs", b)
                after(e, "t_in", b + -1)
                for j in range(TILES):
                    q = e.tensor_scalar(xn[:, j, :], xt[:, b.par, j, :], mv[:, j, 0:1],
                                        rs[:, j:j + 1], ALU.subtract, ALU.mult)
                q.then_inc(s["v_norm"], 1)

            def gru_a(b):
                after(e, "a_u", b)
                after(e, "a_rt", b)
                after(e, "a_nn", b + -1)
                e.scalar_tensor_tensor(out=vv[:, :], in0=rt[:, :], scalar=1.0, in1=uu[:, :],
                                       op0=ALU.add, op1=ALU.mult).then_inc(s["v_v"], 1)
                after(e, "v_v", b)
                after(e, "t_n", b)
                tt(vv[:, :], PI[:, :], vv[:, :], ALU.add, "v_w")

            def gru_d(b):
                after(e, "a_nn", b)
                tt(dd[:, :], xnf[:, b.par], nn[:, :], ALU.subtract, "v_d")

            def gru_b(b):
                after(e, "v_d", b)
                after(e, "a_zt", b)
                e.scalar_tensor_tensor(out=dd[:, :], in0=zt[:, :], scalar=1.0, in1=dd[:, :],
                                       op0=ALU.add, op1=ALU.mult).then_inc(s["v_e"], 1)
                after(e, "v_e", b)
                e.scalar_tensor_tensor(out=dd[:, :], in0=dd[:, :], scalar=0.5, in1=nn[:, :],
                                       op0=ALU.mult, op1=ALU.add).then_inc(s["v_g"], 1)
                after(e, "v_g", b)
                loaded(e, "ld_t", b)
                after(e, "t_x1", b + -1)
                tt(x1[:, :], dd[:, :], xT[:, b.par], ALU.add, "v_x1")

            def nmp_lo(b):
                after(e, "a_nh", b)
                after(e, "t_n", b + -1)
                tt(nl[:, :], PH[:, :], f32(nh[:, :]), ALU.subtract, "v_nl")

            def norm_lo(b):
                after(e, "a_xnh", b)
                after(e, "a_xnf", b)
                after(e, "t_n", b + -2)
                tt(xnl[:, b.par], X0[:, :], f32(xnh[:, b.par]), ALU.subtract, "v_xnl")

            def conv1_lo(b):
                after(e, "a_h1", b)
                after(e, "a_h1h", b)
                after(e, "t_conv2", b + -2)
                tt(h1l[:, b.par, :, PAD:PAD + NODES], h1f[:, :, :],
                   f32(h1h[:, b.par, :, PAD:PAD + NODES]), ALU.subtract, "v_h1l")

            def messages(b):
                after(e, "t_msg", b)
                after(e, "a_msg", b + -1)
                after(e, "v_fac", b + -1)
                half = TILES // 2
                for n, bank in enumerate((PR, X2)):
                    q = e.tensor_tensor(mt[:, n * half:(n + 1) * half, :],
                                        bank[:, 0:half * MSG].rearrange("p (j d) -> p j d", j=half),
                                        bmsg[:, :, :], ALU.add)
                q.then_inc(s["v_mt"], 1)

            def factors(b):
                def left(lo, hi):
                    return fac[:, :, lo:hi]

                def right(lo, hi):
                    return fac[:, :, RIGHT + lo:RIGHT + hi]

                def twice(ap):
                    return f32(ap).unsqueeze(2).broadcast_to([P, TILES, 2, COORDS])

                emb = mt[:, :, D:MSG]
                after(e, "v_mt", b)
                after(e, "t_fac", b + -1)
                e.tensor_copy(right(0, ONCE), emb).then_inc(s["v_s_hi"], 1)
                tt(sq3[:, :, :], emb, emb, ALU.mult, "v_s_sq")
                after(e, "v_s_hi", b)
                tt(right(ONCE, TWICE), emb, f32(right(0, ONCE)), ALU.subtract, "v_s_lo")
                e.tensor_scalar(left(0, TWICE).rearrange("p j (r c) -> p j r c", r=2),
                                twice(right(0, ONCE)), -2.0, None, ALU.mult)
                after(e, "v_s_sq", b)
                e.tensor_reduce(sq[:, :, :], sq3[:, :, :], AX.X, ALU.add).then_inc(s["v_sq"], 1)
                after(e, "v_s_lo", b)
                e.tensor_scalar(left(TWICE, FOUR).rearrange("p j (r c) -> p j r c", r=2),
                                twice(right(ONCE, TWICE)), -2.0, None, ALU.mult)
                after(e, "v_sq", b)
                e.tensor_copy(right(FOUR + 2, FOUR + 3), sq[:, :, :]).then_inc(s["v_sq_hi"], 1)
                e.tensor_copy(right(TWICE, FOUR), f32(right(0, TWICE)))
                after(e, "v_sq_hi", b)
                tt(right(FOUR + 3, FOUR + 4), sq[:, :, :], f32(right(FOUR + 2, FOUR + 3)), ALU.subtract, "v_sq_lo")
                after(e, "v_sq_lo", b)
                e.tensor_copy(left(FOUR, FOUR + 2), f32(right(FOUR + 2, FOUR + 4))).then_inc(s["v_fac"], 1)

            def messages_lo(b):
                after(e, "a_msg", b)
                after(e, "t_av", b + -1)
                tt(ml[:, :], mf[:, :], f32(mh[:, :]), ALU.subtract, "v_ml")

            def weights(b):
                after(e, "a_e1", b)
                loaded(e, "ld_adj", b)
                tt(am[:, :, :], am[:, :, :], adj[:, b.par], ALU.mult, "v_am")

            def weights_lo(b):
                after(e, "a_ah", b)
                after(e, "t_av", b + -1)
                tt(al[:, :, :], am[:, :, :], f32(ah[:, :, :]), ALU.subtract, "v_al")

            def stats2(b, bank=X0):
                after(e, "t_x1", b)
                for j in range(TILES):
                    q = e.bn_stats(st2[:, j, :], bank[:, j * P:(j + 1) * P])
                q.then_inc(s["v_st2"], 1)
                settled(e, "v_st2", b)
                for j in range(TILES):
                    q = e.bn_aggr(mv2[:, j, :], st2[:, j, :])
                q.then_inc(s["v_agg2"], 1)
                after(e, "v_agg2", b)
                after(e, "p_rs2", b + -1)
                e.tensor_scalar(ve2[:, :], mv2[:, :, 1], EPS, None, ALU.add).then_inc(s["v_rs2"], 1)

            def normalize2(b, bank=X0):
                after(e, "p_rs2", b)
                after(e, "a_x1t", b)
                after(e, "t_x2", b + -1)
                early = isinstance(b.k, int) and b.index < 2
                if b.known(2, BLOCKS):
                    e.wait_ge(s[f"sc{b.par}"], 16 * CHOICES * TILES * b.half)
                elif early:
                    e.wait_ge(s["k_sp_dve"], 2)
                for j in range(TILES):
                    q = e.tensor_scalar(rows[:, b.par, 0, j, 0:D], bank[:, j * P:(j + 1) * P],
                                        mv2[:, j, 0:1], rs2[:, j:j + 1], ALU.subtract, ALU.mult)
                q.then_inc(s["v_norm2"], 1)
                to = rows[:, b.par, :, :, D]
                if early:
                    e.tensor_scalar(to, ids[:, b.par], 0.0, None, ALU.add).then_inc(s["v_ids"], 1)
                else:
                    after(e, "v_ids", b + -2)
                    e.tensor_scalar(to, to, 2.0 * BLOCK, None, ALU.add).then_inc(s["v_ids"], 1)

            def conv2_sum(b):
                after(e, "t_conv2", b)
                after(e, "a_c", b + -1)
                e.scalar_tensor_tensor(out=ct[:, :], in0=C2[:, :], scalar=s2[:, 0:1],
                                       in1=xnf[:, b.par], op0=ALU.mult, op1=ALU.add
                                       ).then_inc(s["v_ct"], 1)

            def conv2_lo(b):
                after(e, "a_c", b)
                after(e, "t_n", b + -1)
                tt(cl[:, :], cf[:, :], f32(chh[:, :]), ALU.subtract, "v_cl")

            def choose(b):
                after(e, "t_gate", b)
                sc = X2[:, :].rearrange("p (j n) -> p j n", j=TILES)[:, :, 0:EXPERTS]
                tt(gs[:, :, :], sc, bgate[:, :].rearrange("p (j n) -> p j n", j=TILES), ALU.add, "v_gs")

            def choose_b(b):
                after(e, "v_gs", b)
                shape = [P, TILES, EXPERTS, EXPERTS]
                other = gs[:, :, :].unsqueeze(2).broadcast_to(shape)
                own = gs[:, :, :].unsqueeze(3).broadcast_to(shape)
                tt(cmp_[:, :, :, :], other, own, ALU.is_gt, "v_cmp")
                tt(ceq[:, :, :, :], other, own, ALU.is_equal, "v_ceq")
                after(e, "v_ceq", b)
                tt(ceq[:, :, :, :], ceq[:, :, :, :],
                   earlier[:, :, :].unsqueeze(1).broadcast_to(shape), ALU.mult, "v_sum")
                e.wait_ge(s["v_sum"], 2 * b.index + 1)
                after(e, "v_cmp", b)
                tt(cmp_[:, :, :, :], cmp_[:, :, :, :], ceq[:, :, :, :], ALU.add, "v_sum")
                e.wait_ge(s["v_sum"], 2 * b.index + 2)
                e.tensor_reduce(rank[:, :, :], cmp_[:, :, :, :], AX.X, ALU.add).then_inc(s["v_rank"], 1)
                after(e, "v_rank", b)
                e.tensor_scalar(mask[:, 0:TILES, :], rank[:, :, :], 1.5, None,
                                ALU.is_lt).then_inc(s["v_mask"], 1)

            def place(b):
                after(e, "t_count", b)
                after(e, "v_base", b + -1)
                after(e, "v_sel", b + -1)
                count = X2[:, 0:(TILES + 1) * EXPERTS].rearrange("p (j n) -> p j n", n=EXPERTS)
                tt(pos[:, :, :], count[:, 0:TILES, :],
                   base[:, :].unsqueeze(1).broadcast_to([P, TILES, EXPERTS]), ALU.add, "v_pos")
                after(e, "v_pos", b)
                tt(base[:, :], base[:, :], count[:, TILES, :], ALU.add, "v_base")

            def place_b(b):
                after(e, "v_pos", b)
                if b.known(2, BLOCKS):
                    e.wait_ge(s[f"sc{b.par}"], 16 * CHOICES * TILES * b.half)
                for c in range(CHOICES):
                    q = e.scalar_tensor_tensor(out=sel[:, c], in0=rank[:, :, :], scalar=float(c),
                                               in1=pos[:, :, :], op0=ALU.is_equal, op1=ALU.mult)
                q.then_inc(s["v_sel"], 1)
                after(e, "v_sel", b)
                e.tensor_reduce(row_f[:, :, :], sel[:, :, :, :], AX.X, ALU.add).then_inc(s["v_row"], 1)
                after(e, "v_row", b)
                e.tensor_copy(row_at[:, b.par], row_f[:, :, :]).then_inc(s["v_place"], 1)

            def body(b):
                prev, nxt = b.known(1, BLOCKS + 1), b.known(0, BLOCKS - 1)
                old = b.known(2, BLOCKS)
                if nxt:
                    stats(b + 1)
                if prev:
                    gru_a(b + -1)
                if nxt:
                    normalize(b + 1)
                if old:
                    choose(b + -2)
                    choose_b(b + -2)
                nmp_lo(b)
                if prev:
                    gru_d(b + -1)
                if old:
                    place(b + -2)
                if nxt:
                    norm_lo(b + 1)
                if prev:
                    gru_b(b + -1)
                if old:
                    place_b(b + -2)
                if nxt:
                    messages(b + 1)
                    factors(b + 1)
                    conv1_lo(b + 1)
                if prev:
                    stats2(b + -1)
                if nxt:
                    messages_lo(b + 1)
                if prev:
                    normalize2(b + -1)
                conv2_sum(b)
                if nxt:
                    weights(b + 1)
                conv2_lo(b)
                if nxt:
                    weights_lo(b + 1)

            stats(Block(0, 0))
            e.wait_ge(s["ld_c"], 48)
            e.tensor_scalar(bnv[:, 0:1], vec[:, BN1_V:BN1_V + 1], EPS, None, ALU.add).then_inc(s["k_bn"], 1)
            e.tensor_scalar(bnv[:, 1:2], vec[:, BN2_V:BN2_V + 1], EPS, None, ALU.add).then_inc(s["k_bn"], 1)
            for n, at_b in enumerate((BHH_R, BHH_Z)):
                tt(hb[:, n:n + 1], vec[:, BIH_R + n:BIH_R + n + 1], vec[:, at_b:at_b + 1], ALU.add, "k_hb")
            e.tensor_copy(hb[:, 2:3], vec[:, BHH_N:BHH_N + 1]).then_inc(s["k_hb"], 1)
            e.wait_ge(s["ld_id"], 16)
            e.wait_ge(s["k_hb"], 3)
            e.tensor_scalar(hb[:, :], hb[:, :], 0.5, None, ALU.mult).then_inc(s["k_hb"], 1)
            normalize(Block(0, 0))
            e.wait_ge(s["k_w1"], 1)
            tt(w1c_lo[:, :], raw_w1c, f32(w1c_hi[:, :]), ALU.subtract, "k_sp_dve")
            e.wait_ge(s["k_bnp"], 1)
            tt(s1[:, :], vec[:, BN1_G:BN1_G + 1], bnr[:, 0:1], ALU.mult, "k_bnr")
            tt(s2[:, :], vec[:, BN2_G:BN2_G + 1], bnr[:, 1:2], ALU.mult, "k_bnr")
            e.wait_ge(s["k_bnr"], 2)
            tt(bnt[:, 0:1], vec[:, BN1_M:BN1_M + 1], s1[:, :], ALU.mult, "k_bnr")
            tt(bnt[:, 1:2], vec[:, BN2_M:BN2_M + 1], s2[:, :], ALU.mult, "k_bnr")
            e.wait_ge(s["k_bnr"], 4)
            tt(o1[:, :], vec[:, BN1_B:BN1_B + 1], bnt[:, 0:1], ALU.subtract, "k_bno")
            tt(o2[:, :], vec[:, BN2_B:BN2_B + 1], bnt[:, 1:2], ALU.subtract, "k_bno")
            norm_lo(Block(0, 0))
            e.wait_ge(s["k_ones"], 1)
            messages(Block(0, 0))
            factors(Block(0, 0))
            conv1_lo(Block(0, 0))
            e.wait_ge(s["k_g"], 1)
            tt(w2c_lo[:, :, :].rearrange("p k n -> p (k n)"), raw_w2c,
               f32(w2c_hi[:, :, :].rearrange("p k n -> p (k n)")), ALU.subtract, "k_sp_dve")
            messages_lo(Block(0, 0))
            weights(Block(0, 0))
            weights_lo(Block(0, 0))
            e.wait_ge(s["k_g"], 2)
            tt(wg_lo[:, :, :].rearrange("p k n -> p (k n)"), raw_wg,
               f32(wg_hi[:, :, :].rearrange("p k n -> p (k n)")), ALU.subtract, "k_sp_dve")
            e.wait_ge(s["ld_c2"], 16 * 8)
            e.tensor_copy(before[:, :], before_f[:, :]).then_inc(s["k_id"], 1)
            e.memset(ones[:, :], 1.0).then_inc(s["k_id"], 1)
            e.memset(mask[:, TILES, :], 0.0).then_inc(s["k_id"], 1)
            e.memset(padbase[:, :], 0.0).then_inc(s["k_zero"], 1)
            e.tensor_copy(base[:, :], regbase[:, :]).then_inc(s["k_zero"], 1)
            for n in range(3):
                body(Block(0, n))
            pairs_loop(e, 3, (BLOCKS - 4) // 2, body)
            last = Block(0, BLOCKS - 1)
            body(last)
            gru_a(last)
            choose(last + -1)
            gru_d(last)
            gru_b(last)
            choose_b(last + -1)
            place(last + -1)
            stats2(last)
            place_b(last + -1)
            normalize2(last)
            choose(last)
            choose_b(last)
            place(last)
            place_b(last)

            sizes = [1, EXPERTS, STEPS]
            after(e, "v_base", last)
            e.tensor_copy(end_i[:, :], base[0:1, :]).then_inc(s["k_table"], 1)
            tt(length[:, :], base[0:1, :], regbase[0:1, :], ALU.subtract, "k_tab")
            e.wait_ge(s["k_tab"], 1)
            tt(more[:, :, :], length[:, :].unsqueeze(2).broadcast_to(sizes),
               steps[:, :].unsqueeze(1).broadcast_to(sizes), ALU.is_gt, "k_tab")
            e.wait_ge(s["k_tab"], 2)
            e.tensor_reduce(used[:, :], more[:, :, :], AX.X, ALU.add).then_inc(s["k_tab"], 1)
            e.wait_ge(s["k_tab"], 3)
            tt(usedm[:, :, :], used[:, :].unsqueeze(1).broadcast_to([1, EXPERTS, EXPERTS]),
               earlier[0:1, :, :], ALU.mult, "k_tab")
            e.wait_ge(s["k_tab"], 4)
            e.tensor_reduce(first[:, :], usedm[:, :, :], AX.X, ALU.add).then_inc(s["k_tab"], 1)
            e.wait_ge(s["k_tab"], 5)
            tt(past[:, :], first[:, :], used[:, :], ALU.add, "k_tab")
            sizes = [1, SLOTS, EXPERTS]
            e.wait_ge(s["k_tab"], 6)
            tt(ind[:, :, :], past[:, :].unsqueeze(1).broadcast_to(sizes),
               slotnum[:, :].unsqueeze(2).broadcast_to(sizes), ALU.is_le, "k_tab")
            e.wait_ge(s["k_tab"], 7)
            e.tensor_reduce(whose[:, :], ind[:, :, :], AX.X, ALU.add).then_inc(s["k_tab"], 1)
            tt(indn[:, :, :], ind[:, :, :], used[:, :].unsqueeze(1).broadcast_to(sizes), ALU.mult,
               "k_tab")
            e.wait_ge(s["k_tab"], 9)
            e.tensor_reduce(gone[:, :], indn[:, :, :], AX.X, ALU.add).then_inc(s["k_tab"], 1)
            e.tensor_scalar(whose_i[:, :], whose[:, :], EXPERTS - 1.0, None, ALU.min
                            ).then_inc(s["k_table"], 1)
            e.wait_ge(s["k_tab"], 10)
            tt(gone[:, :], slotnum[:, :], gone[:, :], ALU.subtract, "k_tab")
            e.tensor_scalar(whose[:, :], whose[:, :], float(REGION), None, ALU.mult
                            ).then_inc(s["k_tab"], 1)
            e.wait_ge(s["k_tab"], 12)
            e.scalar_tensor_tensor(out=start[:, :], in0=gone[:, :], scalar=float(BLOCK),
                                   in1=whose[:, :], op0=ALU.mult, op1=ALU.add).then_inc(s["k_tab"], 1)
            e.wait_ge(s["k_tab"], 13)
            e.tensor_copy(start_i[:, :], start[:, :]).then_inc(s["k_table"], 1)
            e.wait_ge(s["k_table"], 3)

            def x_lo(i):
                seen(e, "f_xh", i)
                seen(e, "f_up", i + -2, CH)
                tt(ql[i.par], X0[:, :], f32(qh[i.par]), ALU.subtract, "f_xl")

            def hidden_lo(i):
                for c in range(CH):
                    part = slice(c * BLOCK, (c + 1) * BLOCK)
                    e.wait_ge(s["f_hh"], CH * i.index + c + 1)
                    if c == 0:
                        seen(e, "f_down", i + -2)
                    tt(hl[i.par][:, part], hf[i.par][:, part], f32(hh[i.par][:, part]),
                       ALU.subtract, "f_hl")

            def whose_slot(i):
                n = e.value_load(whose_i[0:1, bass.ds(i.index, 1)], min_val=0, max_val=EXPERTS - 1)
                return n * PICK + B1_AT

            def pick_b1(i):
                n = whose_slot(i)
                seen(e, "f_h", i + -2, CH)
                e.tensor_scalar(b1s[:, i.par], vec[:, bass.ds(n, CH)], 0.0, None, ALU.add
                                ).then_inc(s["f_b1"], 1)

            def pick_b2(i):
                n = whose_slot(i)
                seen(e, "f_y", i + -2)
                e.tensor_scalar(b2s[:, i.par], vec[:, bass.ds(n + CH, 1)], 0.0, None, ALU.add
                                ).then_inc(s["f_b2"], 1)

            def keep_goes(i):
                loaded(e, "f_ld", i)
                seen(e, "f_id", i + -4)
                e.tensor_copy(goes[:, i.quad, :], xr[i.par][:, :, D]).then_inc(s["f_goes"], 1)

            def result_rows(i):
                seen(e, "f_id", i + -1)
                seen(e, "f_pb", i + -1)
                seen(e, "f_goes", i)
                e.tensor_scalar(pad[:, :], goes[:, i.quad], CHOICES * TOKENS - 0.5, padbase[:, 0:1],
                                ALU.is_gt, ALU.mult).then_inc(s["f_isp"], 1)
                seen(e, "f_isp", i)
                if i.known(4, SLOTS):
                    e.wait_ge(s[f"f_sc{i.par}"], 16 * TILES * (i.half - 1))
                tt(result_at[:, i.quad, :], pad[:, :], goes[:, i.quad], ALU.add, "f_id")
                e.tensor_scalar(padbase[:, :], padbase[:, :], float(BLOCK), None, ALU.add
                                ).then_inc(s["f_pb"], 1)

            def y_turned(i):
                seen(e, "f_ty", i)
                if i.known(2, SLOTS):
                    e.wait_ge(s[f"f_sc{i.par}"], 16 * TILES * i.half)
                e.tensor_copy(yt[i.par], turned[i.par][:, :]).then_inc(s["f_yt"], 1)

            def turn(i):
                if i.known(0, SLOTS - 2):
                    x_lo(i + 2)
                    keep_goes(i + 2)
                    pick_b1(i + 2)
                if i.known(1, SLOTS):
                    y_turned(i + -1)
                if i.known(0, SLOTS - 1):
                    hidden_lo(i + 1)
                    pick_b2(i + 1)
                    result_rows(i + 1)

            e.wait_ge(s["k_zero"], 2)
            for n in range(2):
                pick_b1(Slot(0, n))
                x_lo(Slot(0, n))
                keep_goes(Slot(0, n))
            result_rows(Slot(0, 0))
            pick_b2(Slot(0, 0))
            hidden_lo(Slot(0, 0))
            slots(e, turn)
            y_turned(Slot(0, SLOTS - 1))

            e.wait_ge(s["l_x1"], 16 * BLOCKS)
            for c in range(CHUNKS):
                ya, yb = last_y[c % 2]
                e.wait_ge(s[f"l_in{c % 2}"], 16 * CHOICES * (c // 2 + 1))
                tt(ya, ya, yb, ALU.add, "l_y")
                e.wait_ge(s["l_y"], c + 1)
                for h in range(2):
                    x = last_x[2 * c + h]
                    tt(x, x, ya[:, h * BLOCK:(h + 1) * BLOCK], ALU.add, "l_sum")

        @blk.tensor
        def _(e):
            def mm3(o, w_hi, w_lo, m_hi, m_lo, first, end):
                e.matmul(o, w_hi, m_hi, start=first, stop=False)
                e.matmul(o, w_hi, m_lo, start=False, stop=False)
                return e.matmul(o, w_lo, m_hi, start=False, stop=end)

            def conv2(b, lo, hi):
                ps = C2[:, :].rearrange("p (g n) -> p g n", g=GP)
                if lo == 0:
                    after(e, "v_h1l", b)
                    after(e, "a_h1h", b)
                    after(e, "v_ct", b + -1)
                for k in range(lo, hi):
                    m = mm3(ps, w2c_hi[:, k, :], w2c_lo[:, k, :], h1h[:, b.par, :, k:k + NODES],
                            h1l[:, b.par, :, k:k + NODES], k == 0, k == TAPS - 1)
                if hi == TAPS:
                    m.then_inc(s["t_conv2"], 1)

            def message_pass(b):
                after(e, "v_ml", b)
                after(e, "v_al", b)
                after(e, "a_u", b + -1)
                for g in range(GP):
                    for m in range(MB):
                        j = g * MB + m
                        q = mm3(PH[:, g * NODES:(g + 1) * NODES], mh[:, j * P:(j + 1) * P],
                                ml[:, j * P:(j + 1) * P], ah[:, j, :], al[:, j, :], m == 0, m == MB - 1)
                q.then_inc(s["t_av"], 1)

            def turn_in(b):
                after(e, "v_norm", b)
                after(e, "a_x1t", b + -3)
                for j in range(TILES):
                    q = e.transpose(X0[:, j * P:(j + 1) * P], xn[:, j, :], ident[:, :])
                q.then_inc(s["t_in"], 1)

            def conv1(b):
                after(e, "a_xnh", b)
                after(e, "v_xnl", b)
                mm3(X1[:, :], w1c_hi[:, :], w1c_lo[:, :], xnh[:, b.par], xnl[:, b.par], True, True
                    ).then_inc(s["t_conv1"], 1)

            def messages(b):
                after(e, "a_xnf", b)
                after(e, "a_rt", b + -2)
                after(e, "v_base", b + -3)
                half = TILES // 2
                for j in range(TILES):
                    bank, at = (PR, X2)[j // half], j % half * MSG
                    q = e.matmul(bank[:, at:at + MSG], xnf[:, b.par, j * P:(j + 1) * P],
                                 wmsg[:, :], start=True, stop=True)
                q.then_inc(s["t_msg"], 1)

            def turn_factors(b):
                after(e, "v_fac", b)
                after(e, "a_h1", b)
                for j in range(TILES):
                    q = e.transpose(X1[:, j * P:(j + 1) * P], f32(fac[:, j, :]), ident[:, :])
                q.then_inc(s["t_fac"], 1)

            def distances(b):
                after(e, "a_fr", b)
                after(e, "a_zt", b + -2)
                after(e, "v_w", b + -2)
                for g, ps in enumerate((PZ, PI)):
                    for m in range(MB):
                        j = g * MB + m
                        q = e.matmul(ps[:, m * NODES:(m + 1) * NODES], fl[:, j * P:(j + 1) * P],
                                     fr[:, g * NODES:(g + 1) * NODES], start=True, stop=True)
                    q.then_inc(s[f"t_dist{g}"], 1)

            def turn_x1(b, bank=X0):
                after(e, "v_x1", b)
                after(e, "v_xnl", b + 2)
                after(e, "a_xnf", b + 2)
                for j in range(TILES):
                    q = e.transpose(bank[:, j * P:(j + 1) * P], x1[:, j * P:(j + 1) * P], ident[:, :])
                q.then_inc(s["t_x1"], 1)

            def turn_x2(b):
                after(e, "v_norm2", b)
                after(e, "a_fr", b + 2)
                for j in range(TILES):
                    q = e.transpose(X1[:, j * P:(j + 1) * P], rows[:, b.par, 0, j, 0:D], ident[:, :])
                q.then_inc(s["t_x2"], 1)

            def gate(b):
                after(e, "a_x2", b)
                after(e, "v_mt", b + 1)
                after(e, "v_base", b + -1)
                for j in range(TILES):
                    q = e.matmul(X2[:, j * P:(j + 1) * P], x2c[:, j * P:(j + 1) * P], wgate[:, :],
                                 start=True, stop=True)
                q.then_inc(s["t_gate"], 1)

            def gru(b):
                end = isinstance(b.k, int) and b.index == BLOCKS - 1
                xh, xl = xnh[:, b.par], xnl[:, b.par]

                def part(ps, w, g, m_hi, m_lo, first, last):
                    return mm3(ps[:, :], wg_hi[:, w, g * D:(g + 1) * D], wg_lo[:, w, g * D:(g + 1) * D],
                               m_hi, m_lo, first, last)

                if isinstance(b.k, int) and b.index == 0:
                    e.wait_ge(s["k_sp_dve"], 3)
                    e.wait_ge(s["k_g"], 2)
                if end:
                    after(e, "a_rt", b + -1)
                    after(e, "a_zt", b + -1)
                    after(e, "v_w", b + -1)
                after(e, "a_nh", b)
                after(e, "v_nl", b)
                part(PH, 2, 2, xh, xl, True, True).then_inc(s["t_gh"], 1)
                after(e, "v_mt", b + 1)
                part(PR, 2, 0, xh, xl, True, False)
                after(e, "a_e1", b + 1)
                part(PZ, 2, 1, xh, xl, True, False)
                if b.known(1, BLOCKS):
                    turn_x2(b + -1)
                part(PR, 1, 0, nh[:, :], nl[:, :], False, False)
                part(PZ, 1, 1, nh[:, :], nl[:, :], False, False)
                part(PI, 1, 2, nh[:, :], nl[:, :], True, False)
                after(e, "a_ch", b)
                after(e, "v_cl", b)
                part(PR, 0, 0, chh[:, :], cl[:, :], False, True).then_inc(s["t_r"], 1)
                part(PZ, 0, 1, chh[:, :], cl[:, :], False, True).then_inc(s["t_z"], 1)
                part(PI, 0, 2, chh[:, :], cl[:, :], False, True).then_inc(s["t_n"], 1)

            def count(b):
                after(e, "v_mask", b)
                after(e, "v_gs", b)
                n = (TILES + 1) * EXPERTS
                e.matmul(X2[:, 0:n], before[:, :], mask[:, :, :].rearrange("p j n -> p (j n)"),
                         start=True, stop=False)
                for j in range(TILES):
                    q = e.matmul(X2[:, (j + 1) * EXPERTS:n].rearrange("p (r n) -> p r n", n=EXPERTS),
                                 ones[:, :], mask[:, j, :].unsqueeze(1).broadcast_to(
                                     [P, TILES - j, EXPERTS]), start=False, stop=j == TILES - 1)
                q.then_inc(s["t_count"], 1)

            def body(b):
                prev, nxt = b.known(1, BLOCKS + 1), b.known(0, BLOCKS - 1)
                old = b.known(2, BLOCKS)
                if old:
                    gate(b + -2)
                conv2(b, 0, 4)
                message_pass(b)
                conv2(b, 4, 6)
                if nxt:
                    turn_in(b + 1)
                if old:
                    count(b + -2)
                conv2(b, 6, 10)
                if nxt:
                    messages(b + 1)
                    conv1(b + 1)
                conv2(b, 10, 12)
                if prev:
                    turn_x1(b + -1)
                conv2(b, 12, 14)
                if nxt:
                    turn_factors(b + 1)
                conv2(b, 14, 16)
                if nxt:
                    distances(b + 1)
                conv2(b, 16, TAPS)
                gru(b)

            e.wait_ge(s["ld_id"], 16)
            turn_in(Block(0, 0))
            e.wait_ge(s["ld_c"], 48)
            messages(Block(0, 0))
            e.wait_ge(s["k_sp_dve"], 1)
            conv1(Block(0, 0))
            turn_factors(Block(0, 0))
            distances(Block(0, 0))
            e.wait_ge(s["k_sp_dve"], 2)
            e.wait_ge(s["k_g"], 1)
            body(Block(0, 0))
            e.wait_ge(s["ld_c2"], 16 * 8)
            e.wait_ge(s["k_id"], 3)
            body(Block(0, 1))
            body(Block(0, 2))
            pairs_loop(e, 3, (BLOCKS - 4) // 2, body)
            last = Block(0, BLOCKS - 1)
            body(last)

            gate(last + -1)
            count(last + -1)
            turn_x1(last)
            turn_x2(last)
            gate(last)
            count(last)

            def turn_x(i):
                loaded(e, "f_ld", i)
                seen(e, "f_xh", i + -1)
                seen(e, "f_xl", i + -1)
                for j in range(TILES):
                    q = e.transpose(X0[:, j * P:(j + 1) * P], xr[i.par][:, j, 0:D], ident[:, :])
                q.then_inc(s["f_xt"], 1)

            def up_proj(i):
                loaded(e, "f_wu", i)
                seen(e, "f_xh", i)
                seen(e, "f_xl", i)
                seen(e, "f_h", i + -2, CH)
                for c in range(CH):
                    w = wcur[0][i.par][:, :, c * P:(c + 1) * P]
                    mm3(up[i.par][c][:, :], w[:, 0], w[:, 1], qh[i.par], ql[i.par], True, True
                        ).then_inc(s["f_up"], 1)

            def down_proj(i):
                loaded(e, "f_wd", i)
                seen(e, "f_y", i + -1)
                for c in range(CH):
                    w = wcur[1][i.par][:, :, c * D:(c + 1) * D]
                    part = slice(c * BLOCK, (c + 1) * BLOCK)
                    e.wait_ge(s["f_hl"], CH * i.index + c + 1)
                    q = mm3(C2[:, :], w[:, 0], w[:, 1], hh[i.par][:, part], hl[i.par][:, part],
                            c == 0, c == CH - 1)
                q.then_inc(s["f_down"], 1)

            def turn_y(i):
                seen(e, "f_y", i)
                seen(e, "f_yt", i + -2)
                for j in range(TILES):
                    q = e.transpose(turned[i.par][:, j * P:(j + 1) * P], yf[i.par][:, j * P:(j + 1) * P],
                                    ident[:, :])
                q.then_inc(s["f_ty"], 1)

            def turn(i):
                if i.known(0, SLOTS - 2):
                    turn_x(i + 2)
                if i.known(0, SLOTS - 1):
                    up_proj(i + 1)
                if i.known(1, SLOTS):
                    turn_y(i + -1)
                down_proj(i)

            e.wait_ge(s["k_ff"], 4)
            turn_x(Slot(0, 0))
            turn_x(Slot(0, 1))
            up_proj(Slot(0, 0))
            slots(e, turn)
            turn_y(Slot(0, SLOTS - 1))


def kernel(**inputs):
    import numpy as np
    import concourse.bacc as bacc
    from concourse.bass_utils import run_bass_kernel_spmd as run

    v = {k: np.asarray(x) for k, x in inputs.items()}
    gnn = lambda n: v["L0_gnn_" + n]
    ffn = lambda n: v["L0_ffn_" + n]
    w_ih, w_hh = gnn("w_ih"), gnn("w_hh")
    wgate = np.zeros((D, P), np.float32)
    wgate[:, :EXPERTS] = ffn("Wg")
    cols = [gnn(f"bn{n}_{c}") for n in (1, 2) for c in "gbmv"]
    cols += [gnn(w)[n * D:(n + 1) * D] for w in ("b_ih", "b_hh") for n in range(3)]
    for b1, b2 in zip(ffn("b1"), ffn("b2")):
        cols += list(b1.reshape(CH, P)) + [b2]
    token = np.arange(2 * BLOCK).reshape(2, 1, TILES, P).transpose(3, 0, 1, 2)
    padding = np.zeros((BLOCK, ROW), np.float32)
    padding[:, D] = CHOICES * TOKENS + np.arange(BLOCK)
    arrays = {
        "x": v["x"].reshape(TOKENS, D),
        "xT": v["x"].reshape(TOKENS, D).T,
        "adjT": v["adj"].transpose(0, 2, 1).reshape(TOKENS, NODES),
        "conv1": gnn("conv1_w")[:, :, 0].T,
        "conv2": gnn("conv2_w").transpose(1, 2, 0).reshape(D, TAPS * D),
        "wgru": np.concatenate([w_ih[:, :D].T, w_ih[:, D:].T, w_hh.T], axis=1),
        "wmsg": np.concatenate([gnn("w_msg").T, gnn("w_se").T], axis=1),
        "wgate": wgate,
        "wup": ffn("W1").transpose(1, 0, 2).reshape(D, EXPERTS * HID),
        "wdown": ffn("W2").reshape(EXPERTS, CH, P, D).transpose(2, 0, 1, 3).reshape(P, -1),
        "vec": np.stack(cols, axis=1),
        "bmsg": np.broadcast_to(np.concatenate([gnn("b_msg"), gnn("b_se")]), (P, TILES // 2, MSG)),
        "bgate": np.broadcast_to(np.tile(ffn("bg"), TILES), (P, TILES * EXPERTS)),
        "ident": np.eye(P, dtype=np.float32),
        "earlier": np.broadcast_to(np.tril(np.ones((EXPERTS, EXPERTS), np.float32), -1),
                                   (P, EXPERTS, EXPERTS)),
        "before": np.triu(np.ones((P, P), np.float32), 1),
        "regbase": np.broadcast_to(np.arange(EXPERTS, dtype=np.float32) * REGION, (P, EXPERTS)),
        "steps": np.arange(STEPS, dtype=np.float32)[None] * BLOCK,
        "slotnum": np.arange(SLOTS, dtype=np.float32)[None],
        "ids": np.concatenate([token, token + TOKENS], axis=2).astype(np.float32),
        "padding": padding,
    }
    arrays = {k: np.ascontiguousarray(x) for k, x in arrays.items()}
    nc = bacc.Bacc("TRN2", target_bir_lowering=False, num_devices=1)
    aps = {k: nc.dram_tensor(f"in_{k}", x.shape, mybir.dt.from_np(x.dtype), kind="ExternalInput").ap()
           for k, x in arrays.items()}
    out = nc.dram_tensor("out", [TOKENS, D], F32, kind="ExternalOutput").ap()
    build(nc, aps, out)
    r = run(nc, [{f"in_{k}": x for k, x in arrays.items()}], core_ids=[0])
    return r.results[0]["out"].reshape(GRAPHS, NODES, D)
```
